# Optimizing a Trainium2 kernel written in Bass

```python
import numpy as np
import jax
import jax.numpy as jnp

def _softmax(x, axis=-1):
    return jax.nn.softmax(x, axis=axis)

def _gelu(x):
    return jax.nn.gelu(x, approximate=True)

def _silu(x):
    return jax.nn.silu(x)

def _sigmoid(x):
    return jax.nn.sigmoid(x)

def _layernorm(x, axis=-1, eps=1e-05):
    m = jnp.mean(x, axis=axis, keepdims=True)
    v = jnp.var(x, axis=axis, keepdims=True)
    return (x - m) / jnp.sqrt(v + eps)

def _scatter_add(tgt, idx, src, axis=0):
    return tgt.at[idx].add(src)

def _segment_sum(src, seg, n):
    return jax.ops.segment_sum(src, seg, n)
kernel_name = 'mk_pixart_resid_d2_seqx_r8_27b010'

def setup_inputs(seed: int=0):
    np.random.seed(seed)
    _w = jnp.asarray

    def _rec_inputs():
        import jax
        import jax.numpy as jnp
        _rk = jax.random.key(seed)
        x = 7.22e-05 + 1 * jax.random.normal(jax.random.fold_in(_rk, 1), (16, 128, 128), jnp.float32)
        _lenS = 128 - jax.random.randint(jax.random.fold_in(_rk, 7), (16,), 0, max(1, 128 // 4) + 1, jnp.int32)
        _lenS2 = 128 - jax.random.randint(jax.random.fold_in(_rk, 8), (16,), 0, max(1, 128 // 4) + 1, jnp.int32)
        _ctx_1024P = jax.random.normal(jax.random.fold_in(_rk, 11), (16, 16, 128), jnp.float32)
        _ctx_1024c = jax.random.dirichlet(jax.random.fold_in(_rk, 511), 0.3 * jnp.ones((16,), jnp.float32), (16, 128))
        _ctx_1024t = jnp.einsum('bsk,bkd->bsd', _ctx_1024c, _ctx_1024P)
        _ctx_1024t = _ctx_1024t * jax.lax.rsqrt(jnp.mean(jnp.square(_ctx_1024t)) + 1e-12) * 0.953939
        ctx_1024 = 4.13588e-05 + 0.999923 * (_ctx_1024t + 0.3 * jax.random.normal(jax.random.fold_in(_rk, 611), (16, 128, 128), jnp.float32))
        condB_tau = jax.random.uniform(jax.random.fold_in(_rk, 12), (16,), jnp.float32, 0.0, 1.45372)
        fside_BxS2_0 = 0.0088954 + 1.00633 * jax.random.normal(jax.random.fold_in(_rk, 13), (16, 128), jnp.float32)
        return (x, ctx_1024, condB_tau, fside_BxS2_0)
    x, ctx_1024, condB_tau, fside_BxS2_0 = _rec_inputs()

    def _L0_xcond_setup():
        import jax, jax.numpy as jnp
        import numpy as np
        D_MODEL = 128
        N_HEADS = 16
        key = jax.random.key(seed)
        ks = jax.random.split(key, 16)
        B, L, S, D = (4, 256, 256, D_MODEL)
        inp = {'q': jax.random.normal(ks[0], (B, L, D), jnp.float32), 'k': jax.random.normal(ks[1], (B, S, D), jnp.float32), 'v': jax.random.normal(ks[2], (B, S, D), jnp.float32), 'tau': jax.random.uniform(ks[3], (B, 1), jnp.float32, 0.5, 1.5), 'delta': jax.random.normal(ks[4], (B, S), jnp.float32)}
        s = 1.0 / np.sqrt(D)
        inp['Wq'] = jax.random.normal(ks[5], (D, D), jnp.float32) * s
        inp['bq'] = jnp.zeros((D,), jnp.float32)
        inp['Wk'] = jax.random.normal(ks[6], (D, D), jnp.float32) * s
        inp['bk'] = jnp.zeros((D,), jnp.float32)
        inp['Wv'] = jax.random.normal(ks[7], (D, D), jnp.float32) * s
        inp['bv'] = jnp.zeros((D,), jnp.float32)
        inp['Wo'] = jax.random.normal(ks[8], (D, D), jnp.float32) * s
        inp['bo'] = jnp.zeros((D,), jnp.float32)
        return inp
    _L0_xcond_all = _L0_xcond_setup()
    _L0_xcond_in = {k: v for k, v in _L0_xcond_all.items() if k in ('Wq', 'bq', 'Wk', 'bk', 'Wv', 'bv', 'Wo', 'bo')}
    del _L0_xcond_all

    def _L0_ffn_setup():
        import jax, jax.numpy as jnp
        import numpy as np
        D_MODEL, D_FF, N_EXPERTS, TOP_K = (128, 512, 8, 2)
        key = jax.random.key(seed)
        k0, k1, k2, k3 = jax.random.split(key, 4)
        x = jax.random.normal(k0, (2, 256, D_MODEL), dtype=jnp.float32)
        Wg = jax.random.normal(k1, (D_MODEL, N_EXPERTS), dtype=jnp.float32) * 0.02
        W1 = jax.random.normal(k2, (N_EXPERTS, D_MODEL, D_FF), dtype=jnp.float32) * 0.02
        b1 = jnp.zeros((N_EXPERTS, D_FF), dtype=jnp.float32)
        W2 = jax.random.normal(k3, (N_EXPERTS, D_FF, D_MODEL), dtype=jnp.float32) * 0.02
        b2 = jnp.zeros((N_EXPERTS, D_MODEL), dtype=jnp.float32)
        return {'x': x, 'Wg': Wg, 'W1': W1, 'b1': b1, 'W2': W2, 'b2': b2}
    _L0_ffn_all = _L0_ffn_setup()
    _L0_ffn_in = {k: v for k, v in _L0_ffn_all.items() if k in ('Wg', 'W1', 'b1', 'W2', 'b2')}
    del _L0_ffn_all

    def _L1_xcond_setup():
        import jax, jax.numpy as jnp
        import numpy as np
        B, S, D, H = (2, 256, 128, 16)
        DK = D // H

        def _split_heads(x):
            b, s, _ = x.shape
            return x.reshape(b, s, H, DK).transpose(0, 2, 1, 3)
        key = jax.random.key(seed)
        ks = jax.random.split(key, 14)
        inp = {'query': jax.random.normal(ks[0], (B, S, D), jnp.float32), 'key': jax.random.normal(ks[1], (B, S, D), jnp.float32), 'value': jax.random.normal(ks[2], (B, S, D), jnp.float32), 'tau': jax.random.uniform(ks[3], (B, 1), jnp.float32, 0.5, 1.5), 'delta': jax.random.normal(ks[4], (B, S), jnp.float32)}
        sc = 1.0 / np.sqrt(D)
        for i, name in enumerate(['q', 'k', 'v', 'o']):
            inp[f'W{name}'] = jax.random.normal(ks[5 + 2 * i], (D, D), jnp.float32) * sc
            inp[f'b{name}'] = jax.random.normal(ks[6 + 2 * i], (D,), jnp.float32) * 0.01
        return inp
    _L1_xcond_all = _L1_xcond_setup()
    _L1_xcond_in = {k: v for k, v in _L1_xcond_all.items() if k in ('Wq', 'bq', 'Wk', 'bk', 'Wv', 'bv', 'Wo', 'bo')}
    del _L1_xcond_all

    def _L1_ffn_setup():
        import jax, jax.numpy as jnp
        import numpy as np
        B, T, D, H, E, K = (2, 256, 128, 512, 8, 2)
        EPS = 1e-12

        def moe_forward(x, Wg, bg, W1, b1, W2, b2):
            gates = jax.nn.softmax(x @ Wg + bg, axis=-1)
            _, top_idx = jax.lax.top_k(gates, K)
            mask = jax.nn.one_hot(top_idx, E, dtype=gates.dtype).sum(axis=-2)
            g = gates * mask
            g = g / jnp.maximum(jnp.sum(jnp.abs(g), axis=-1, keepdims=True), EPS)
            h = jnp.einsum('btd,edh->bteh', x, W1) + b1[None, None]
            h = jax.nn.gelu(h, approximate=False)
            eo = jnp.einsum('bteh,ehd->bted', h, W2) + b2[None, None]
            return jnp.einsum('bte,bted->btd', g, eo)
        key = jax.random.key(seed)
        ks = jax.random.split(key, 8)
        s_d = 1.0 / np.sqrt(D)
        s_h = 1.0 / np.sqrt(H)
        return {'x': jax.random.normal(ks[0], (B, T, D), dtype=jnp.float32), 'Wg': jax.random.uniform(ks[1], (D, E), jnp.float32, -s_d, s_d), 'bg': jax.random.uniform(ks[2], (E,), jnp.float32, -s_d, s_d), 'W1': jax.random.uniform(ks[3], (E, D, H), jnp.float32, -s_d, s_d), 'b1': jax.random.uniform(ks[4], (E, H), jnp.float32, -s_d, s_d), 'W2': jax.random.uniform(ks[5], (E, H, D), jnp.float32, -s_h, s_h), 'b2': jax.random.uniform(ks[6], (E, D), jnp.float32, -s_h, s_h)}
    _L1_ffn_all = _L1_ffn_setup()
    _L1_ffn_in = {k: v for k, v in _L1_ffn_all.items() if k in ('Wg', 'bg', 'W1', 'b1', 'W2', 'b2')}
    del _L1_ffn_all
    return {'x': x, 'ctx_1024': ctx_1024, 'condB_tau': condB_tau, 'fside_BxS2_0': fside_BxS2_0, 'L0_xcond_Wq': _L0_xcond_in['Wq'], 'L0_xcond_bq': _L0_xcond_in['bq'], 'L0_xcond_Wk': _L0_xcond_in['Wk'], 'L0_xcond_bk': _L0_xcond_in['bk'], 'L0_xcond_Wv': _L0_xcond_in['Wv'], 'L0_xcond_bv': _L0_xcond_in['bv'], 'L0_xcond_Wo': _L0_xcond_in['Wo'], 'L0_xcond_bo': _L0_xcond_in['bo'], 'L0_ffn_Wg': _L0_ffn_in['Wg'], 'L0_ffn_W1': _L0_ffn_in['W1'], 'L0_ffn_b1': _L0_ffn_in['b1'], 'L0_ffn_W2': _L0_ffn_in['W2'], 'L0_ffn_b2': _L0_ffn_in['b2'], 'L1_xcond_Wq': _L1_xcond_in['Wq'], 'L1_xcond_bq': _L1_xcond_in['bq'], 'L1_xcond_Wk': _L1_xcond_in['Wk'], 'L1_xcond_bk': _L1_xcond_in['bk'], 'L1_xcond_Wv': _L1_xcond_in['Wv'], 'L1_xcond_bv': _L1_xcond_in['bv'], 'L1_xcond_Wo': _L1_xcond_in['Wo'], 'L1_xcond_bo': _L1_xcond_in['bo'], 'L1_ffn_Wg': _L1_ffn_in['Wg'], 'L1_ffn_bg': _L1_ffn_in['bg'], 'L1_ffn_W1': _L1_ffn_in['W1'], 'L1_ffn_b1': _L1_ffn_in['b1'], 'L1_ffn_W2': _L1_ffn_in['W2'], 'L1_ffn_b2': _L1_ffn_in['b2']}

def reference(x, ctx_1024, condB_tau, fside_BxS2_0, L0_xcond_Wq, L0_xcond_bq, L0_xcond_Wk, L0_xcond_bk, L0_xcond_Wv, L0_xcond_bv, L0_xcond_Wo, L0_xcond_bo, L0_ffn_Wg, L0_ffn_W1, L0_ffn_b1, L0_ffn_W2, L0_ffn_b2, L1_xcond_Wq, L1_xcond_bq, L1_xcond_Wk, L1_xcond_bk, L1_xcond_Wv, L1_xcond_bv, L1_xcond_Wo, L1_xcond_bo, L1_ffn_Wg, L1_ffn_bg, L1_ffn_W1, L1_ffn_b1, L1_ffn_W2, L1_ffn_b2):
    import jax
    import jax.numpy as jnp

    def _L0_xcond_ref(q, k, v, tau, delta, Wq, bq, Wk, bk, Wv, bv, Wo, bo):
        import jax, jax.numpy as jnp
        import numpy as np
        D_MODEL = 128
        N_HEADS = 16
        B, L, D = q.shape
        S = k.shape[1]
        H = N_HEADS
        E = D // H
        qh = (q @ Wq.T + bq).reshape(B, L, H, E)
        kh = (k @ Wk.T + bk).reshape(B, S, H, E)
        vh = (v @ Wv.T + bv).reshape(B, S, H, E)
        scale = 1.0 / np.sqrt(E).astype(np.float32)
        scores = jnp.einsum('blhe,bshe->bhls', qh, kh)
        scores = scores * tau[:, None, None, :] + delta[:, None, None, :]
        a = jax.nn.softmax(scale * scores, axis=-1)
        out = jnp.einsum('bhls,bshd->blhd', a, vh).reshape(B, L, D)
        return out @ Wo.T + bo

    def _L0_ffn_ref(x, Wg, W1, b1, W2, b2):
        import jax, jax.numpy as jnp
        import numpy as np
        D_MODEL, D_FF, N_EXPERTS, TOP_K = (128, 512, 8, 2)
        B = x.shape[:-1]
        xs = x.reshape(-1, x.shape[-1])
        T = xs.shape[0]
        gate_logits = xs @ Wg
        weights, sel = jax.lax.top_k(gate_logits, TOP_K)
        weights = jax.nn.softmax(weights.astype(jnp.float32), axis=1).astype(x.dtype)
        h = jax.nn.relu(jnp.einsum('td,edf->etf', xs, W1) + b1[:, None, :])
        out_e = jnp.einsum('etf,efd->etd', h, W2) + b2[:, None, :]
        tok = jnp.arange(T)
        picked = out_e[sel, tok[:, None]]
        out = jnp.einsum('tk,tkd->td', weights, picked)
        return out.reshape(*B, x.shape[-1])

    def _L1_xcond_ref(query, key, value, tau, delta, Wq, bq, Wk, bk, Wv, bv, Wo, bo):
        import jax, jax.numpy as jnp
        import numpy as np
        B, S, D, H = (2, 256, 128, 16)
        DK = D // H

        def _split_heads(x):
            b, s, _ = x.shape
            return x.reshape(b, s, H, DK).transpose(0, 2, 1, 3)
        q = _split_heads(query @ Wq.T + bq)
        k = _split_heads(key @ Wk.T + bk)
        v = _split_heads(value @ Wv.T + bv)
        scores = jnp.einsum('bhqd,bhkd->bhqk', q, k)
        scores = scores * tau[:, :, None, None] + delta[:, None, None, :]
        scores = scores / jnp.sqrt(jnp.asarray(DK, scores.dtype))
        p_attn = jax.nn.softmax(scores, axis=-1)
        x = jnp.einsum('bhqk,bhkd->bhqd', p_attn, v)
        x = x.transpose(0, 2, 1, 3).reshape(query.shape[0], -1, H * DK)
        return x @ Wo.T + bo

    def _L1_ffn_ref(x, Wg, bg, W1, b1, W2, b2):
        import jax, jax.numpy as jnp
        import numpy as np
        B, T, D, H, E, K = (2, 256, 128, 512, 8, 2)
        EPS = 1e-12

        def moe_forward(x, Wg, bg, W1, b1, W2, b2):
            gates = jax.nn.softmax(x @ Wg + bg, axis=-1)
            _, top_idx = jax.lax.top_k(gates, K)
            mask = jax.nn.one_hot(top_idx, E, dtype=gates.dtype).sum(axis=-2)
            g = gates * mask
            g = g / jnp.maximum(jnp.sum(jnp.abs(g), axis=-1, keepdims=True), EPS)
            h = jnp.einsum('btd,edh->bteh', x, W1) + b1[None, None]
            h = jax.nn.gelu(h, approximate=False)
            eo = jnp.einsum('bteh,ehd->bted', h, W2) + b2[None, None]
            return jnp.einsum('bte,bted->btd', g, eo)
        return moe_forward(x, Wg, bg, W1, b1, W2, b2)
    x = x + _L0_xcond_ref(_layernorm(x, axis=-1), ctx_1024, ctx_1024, condB_tau[:, None], fside_BxS2_0, L0_xcond_Wq, L0_xcond_bq, L0_xcond_Wk, L0_xcond_bk, L0_xcond_Wv, L0_xcond_bv, L0_xcond_Wo, L0_xcond_bo)
    x = x + _L0_ffn_ref(_layernorm(x, axis=-1), L0_ffn_Wg, L0_ffn_W1, L0_ffn_b1, L0_ffn_W2, L0_ffn_b2)
    x = x + _L1_xcond_ref(_layernorm(x, axis=-1), ctx_1024, ctx_1024, condB_tau[:, None], fside_BxS2_0, L1_xcond_Wq, L1_xcond_bq, L1_xcond_Wk, L1_xcond_bk, L1_xcond_Wv, L1_xcond_bv, L1_xcond_Wo, L1_xcond_bo)
    x = x + _L1_ffn_ref(_layernorm(x, axis=-1), L1_ffn_Wg, L1_ffn_bg, L1_ffn_W1, L1_ffn_b1, L1_ffn_W2, L1_ffn_b2)
    return x

_drawn_inputs = setup_inputs


def setup_inputs(seed=0):
    import zlib

    import numpy as np

    out = dict(_drawn_inputs(seed))
    spreads = {'L0_xcond_bq': (0.0, 0.407),
     'L0_xcond_bk': (0.0, 2.0),
     'L0_xcond_bv': (0.0, 0.1),
     'L0_xcond_bo': (0.0, 0.1),
     'L0_ffn_b1': (0.0, 0.341),
     'L0_ffn_b2': (0.0, 0.1)}
    factors = {'L1_xcond_bq': 27.34,
     'L1_xcond_bk': 64.0,
     'L1_xcond_bv': 4.776,
     'L1_xcond_bo': 5.634,
     'L1_ffn_b1': 5.384,
     'L1_ffn_b2': 3.86}
    for name, (base, spread) in spreads.items():
        noise = np.random.default_rng([zlib.crc32(name.encode()), seed]).standard_normal(out[name].shape)
        drawn = base * np.exp(spread * noise) if base else spread * noise
        out[name] = jnp.asarray(drawn.astype(out[name].dtype))
    for name, factor in factors.items():
        out[name] = (out[name] * factor).astype(out[name].dtype)
    return out
```

```python
from contextlib import ExitStack

import numpy as np

import concourse.bass as bass
from concourse import mybir

F32 = mybir.dt.float32
F32R = mybir.dt.float32r
ALU = mybir.AluOpType
ACT = mybir.ActivationFunctionType
AX = mybir.AxisListType

P = 128
LAYERS = 2
BATCHES = 16
GROUP = 4
GROUPS = BATCHES // GROUP
GT = GROUP * P
TOKENS = BATCHES * P
HEADS = 16
HD = P // HEADS
HG = 4
HROWS = P // HG
UNITS = HG
EXPERTS = 8
FF = 512
FC = FF // P
LN_EPS = 1e-5
GATE_EPS = 1e-12
SOFTMAX_SCALE = 1.0 / float(np.sqrt(HD))
MISC_BANKS = 3
H_BANKS = 4
Y_BANKS = 2
ROW_ONE, ROW_MAX = 3 * HD, 3 * HD + 2
B1_ROWS = EXPERTS * FC
MISC = ("wT", "rT", "ctxT", "xT1", "qp", "kp", "vp", "qs", "ks", "mT", "oT", "wo", "xT2", "lg", "gT", "b2")


def attention_order(layer):
    def prepare(g):
        first = [("ctxT", layer, g)] if layer == 0 else []
        return [first + [("xT1", layer, g), ("kp", layer, g)],
                [("qp", layer, g), ("vp", layer, g), ("ks", layer, g, 0), ("ks", layer, g, 1)],
                [("ks", layer, g, 2), ("ks", layer, g, 3)] + [("qs", layer, g, j) for j in range(HG)]]

    yield ("ln1", layer, 0)
    for part in prepare(0):
        yield from part
    for i in range(UNITS):
        yield ("A", layer, 0, i)
    yield ("mT", layer, 0)
    yield ("ln1", layer, 1)
    for s in range(BATCHES + 5):
        for i in range(UNITS):
            if s + 1 < BATCHES:
                yield ("A", layer, s + 1, i)
            if s < BATCHES:
                yield ("B", layer, s, i)
            if 1 <= s <= BATCHES:
                yield ("PV", layer, s - 1, i)
        if 2 <= s < BATCHES + 2:
            yield ("wo", layer, s - 2)
        g, r = s // GROUP + 1, s % GROUP
        if g < GROUPS and r < 3:
            yield from prepare(g)[r]
        if s + 1 < BATCHES:
            yield ("mT", layer, s + 1)
        if 1 <= s <= BATCHES:
            yield ("oT", layer, s - 1)
        if g + 1 < GROUPS and r == 3:
            yield ("ln1", layer, g + 1)
        for name, at in (("ln2", 5), ("xT2", 6), ("lg", 7), ("gT", 8), ("b2", 8)):
            if s >= at and (s - at) % GROUP == 0 and (s - at) // GROUP < GROUPS:
                yield (name, layer, (s - at) // GROUP)


ORDER = [list(attention_order(layer)) for layer in range(LAYERS)]
USES = [("wT", layer) for layer in range(LAYERS)] + [("rT",)]
USES += [p for order in ORDER for p in order if p[0] in MISC]
MISC_USE = {piece: n for n, piece in enumerate(USES)}


def build(nc, x, ctx_in, tau, delta, wts, b1, bqk, bv, bo, wg, bg, w1, w2, b2, out):
    stack = ExitStack()
    with stack:
        def sb(name, shape, dt=F32):
            return stack.enter_context(nc.sbuf_tensor(name, shape, dt))

        def sem(name):
            return stack.enter_context(nc.semaphore(name))

        def f32(ap):
            return ap.bitcast(F32)

        X = sb("X", [P, BATCHES, P])
        ctx_raw = sb("ctx_raw", [P, BATCHES, P])
        ctx_hi, ctx_lo = sb("ctx_hi", [P, TOKENS], F32R), sb("ctx_lo", [P, TOKENS], F32R)
        xt_hi, xt_lo = sb("xt_hi", [P, TOKENS], F32R), sb("xt_lo", [P, TOKENS], F32R)
        w_raw = sb("w_raw", [P, LAYERS, 4, P])
        w_hi, w_lo = sb("w_hi", [P, LAYERS, 4, P], F32R), sb("w_lo", [P, LAYERS, 4, P], F32R)
        rows_raw = sb("rows_raw", [P, P])
        cols = sb("cols", [P, P])
        N_ROWS = LAYERS * (B1_ROWS + 2)
        ident = sb("ident", [P, P])
        zeros = sb("zeros", [P, P])
        one_cols = sb("one_cols", [P, 2])
        sel_q_hi, sel_q_lo = sb("sel_q_hi", [P, HG, P], F32R), sb("sel_q_lo", [P, HG, P], F32R)
        sel_k_hi, sel_k_lo = sb("sel_k_hi", [P, HG, P], F32R), sb("sel_k_lo", [P, HG, P], F32R)
        tau_sc = sb("tau_sc", [P, BATCHES])
        tau_raw = sb("tau_raw", [P, BATCHES])
        delta_raw = sb("delta_raw", [BATCHES, P])
        delta_sc = sb("delta_sc", [BATCHES, P])
        delta_hi, delta_lo = sb("delta_hi", [BATCHES, P], F32R), sb("delta_lo", [BATCHES, P])
        k_extra = sb("k_extra", [P, TOKENS])
        bv_all, bo_all = sb("bv_all", [P, LAYERS, P]), sb("bo_all", [P, LAYERS, P])
        wg_raw = sb("wg_raw", [P, LAYERS, EXPERTS])
        wg_hi, wg_lo = sb("wg_hi", [P, LAYERS, EXPERTS], F32R), sb("wg_lo", [P, LAYERS, EXPERTS], F32R)
        bg_all = sb("bg_all", [P, EXPERTS])
        b2_sb = sb("b2_sb", [EXPERTS, LAYERS, P])
        lower = sb("lower", [P, EXPERTS, EXPERTS])
        stats, mv = sb("stats", [P, GROUP, 6]), sb("mv", [P, GROUP, 2])
        var_eps, rstd = sb("var_eps", [P, GROUP]), sb("rstd", [P, GROUP])
        minus_half = sb("minus_half", [P, GROUP])
        xn = sb("xn", [P, GROUP, P])
        full = sb("full", [P, 2, GT])
        part_hi, part_lo = sb("part_hi", [P, 2, GT], F32R), sb("part_lo", [P, 2, GT], F32R)
        big = sb("big", [P, 2, 2, HG, GT], F32R)
        q2 = sb("q2", [P, 2, HG, P], F32R)
        probs = sb("probs", [P, 2, UNITS, HG, P])
        v_sb = sb("v_sb", [P, 2, GROUP, HEADS, HD + 1])
        neg_max = sb("neg_max", [P, HEADS])
        max_cols = sb("max_cols", [P, HG, P])
        rec = sb("rec", [P, HEADS])
        attn = sb("attn", [P, P])
        attn_hi, attn_lo = sb("attn_hi", [P, 2, P], F32R), sb("attn_lo", [P, 2, P], F32R)
        logits, shifted = sb("logits", [P, GROUP, EXPERTS]), sb("shifted", [P, GROUP, EXPERTS])
        expd, numer = sb("expd", [P, GROUP, EXPERTS]), sb("numer", [P, GROUP, EXPERTS])
        gsmall = sb("gsmall", [P, 6, GROUP])
        cmp_gt, cmp_eq = (sb(n, [P, GROUP, EXPERTS, EXPERTS]) for n in ("cmp_gt", "cmp_eq"))
        rank = sb("rank", [P, GROUP, EXPERTS])
        gates = sb("gates", [P, EXPERTS, BATCHES])
        gates_t = sb("gates_t", [EXPERTS, GT])
        w1_raw, w2_raw = sb("w1_raw", [P, 2, FF]), sb("w2_raw", [P, 2, FC, P])
        w1_hi, w1_lo = sb("w1_hi", [P, 2, FF], F32R), sb("w1_lo", [P, 2, FF], F32R)
        w2_hi, w2_lo = sb("w2_hi", [P, 2, FC, P], F32R), sb("w2_lo", [P, 2, FC, P], F32R)
        hidden = sb("hidden", [P, 2, GT])

        bank = [stack.enter_context(nc.psum_tensor(f"bank{n}", [P, 512], F32)) for n in range(8)]
        a_bank, b_bank, pv_bank, misc_bank = bank[0:2], bank[2:4], bank[4], bank[5:8]
        h_bank, y_bank = bank[0:4], [bank[4], bank[7]]

        in_small, in_w = sem("in_small"), sem("in_w")
        in_x = [sem(f"in_x{g}") for g in range(GROUPS)]
        in_ctx = [sem(f"in_ctx{g}") for g in range(GROUPS)]
        in_rows, out_done = sem("in_rows"), sem("out_done")
        const_ready = sem("const_ready")
        sel_ready = sem("sel_ready")
        delta_ready, extra_ready = sem("delta_ready"), sem("extra_ready")
        misc_full = sem("misc_full")
        misc_done = [sem(f"misc_done{n}") for n in range(MISC_BANKS)]
        hi_ready = sem("hi_ready")
        var_ready, rstd_ready = sem("var_ready"), sem("rstd_ready")
        xn_ready, bo_added = sem("xn_ready"), sem("bo_added")
        full_ready, part_hi_ready, part_lo_ready = sem("full_ready"), sem("part_hi_ready"), sem("part_lo_ready")
        a_full, a_free, b_full, b_free = sem("a_full"), sem("a_free"), sem("b_full"), sem("b_free")
        max_ready = sem("max_ready")
        pv_full, pv_free, attn_ready = sem("pv_full"), sem("pv_free"), sem("attn_ready")
        shifted_ready, exp_ready, gates_ready = sem("shifted_ready"), sem("exp_ready"), sem("gates_ready")
        dve_step, act_step, pool_step = sem("dve_step"), sem("act_step"), sem("pool_step")
        pool_waits = sem("pool_waits")
        w_load = [sem(f"w_load{s}") for s in range(2)]
        w_ready = sem("w_ready")
        h_full, h_free = sem("h_full"), sem("h_free")
        hh_ready, hl_ready = sem("hh_ready"), sem("hl_ready")
        y_full, y_free = sem("y_full"), sem("y_free")

        def hidden_part(part, slot):
            return big[:, slot, part, :, :]

        def q_tile(g):
            return big[:, g % 2, 0, :, :]

        def k_tile(g):
            return big[:, g % 2, 1, :, :]

        def misc(piece):
            n = MISC_USE[piece]
            return misc_bank[n % MISC_BANKS], n

        def wait_full(eng, n):
            eng.wait_ge(misc_full, n + 1)

        def wait_done(eng, piece):
            n = MISC_USE[piece]
            eng.wait_ge(misc_done[n % MISC_BANKS], n // MISC_BANKS + 1)

        def done(n):
            return misc_done[n % MISC_BANKS]

        UPL = BATCHES * UNITS
        HPL = EXPERTS * GROUPS * FC
        YPL = EXPERTS * GROUPS

        def uses_before(layer, kind, g, k=0):
            return (layer * GROUPS + g) * 2 + k

        block = stack.enter_context(nc.Block())

        @block.sync
        def _(sp):
            for layer in range(LAYERS):
                for k in range(4):
                    sp.dma_start(w_raw[:, layer, k, :], wts[layer][k]).then_inc(in_w, 16)
            for layer in range(LAYERS):
                sp.dma_start(rows_raw[layer * B1_ROWS:(layer + 1) * B1_ROWS, :],
                             b1[layer].rearrange("e (c p) -> (e c) p", p=P)).then_inc(in_rows, 16)
                for k in range(2):
                    r = LAYERS * B1_ROWS + 2 * layer + k
                    sp.dma_start(rows_raw[r:r + 1, :], bqk[layer][k].rearrange("(a n) -> a n", a=1)).then_inc(in_rows, 16)
            for g in range(GROUPS):
                bs = slice(g * GROUP, (g + 1) * GROUP)
                sp.dma_start(X[:, bs, :], x[bs].rearrange("b t d -> t b d")).then_inc(in_x[g], 16)
                sp.dma_start(ctx_raw[:, bs, :], ctx_in[bs].rearrange("b t d -> t b d")).then_inc(in_ctx[g], 16)

            def load_expert(layer, e, slot):
                sp.dma_start(w1_raw[:, slot, :], w1[layer][e]).then_inc(w_load[slot], 16)
                sp.dma_start(w2_raw[:, slot, :, :], w2[layer][e].rearrange("(c p) d -> p c d", p=P)).then_inc(w_load[slot], 16)

            for slot in range(2):
                load_expert(0, slot, slot)
            sp.wait_ge(delta_ready, 2)
            for i in range(HG):
                for k, src in enumerate((f32(delta_hi[:, :]), delta_lo[:, :])):
                    r = HROWS * i + ROW_ONE + k
                    sp.dma_start(k_extra[r:r + 1, :], src).then_inc(extra_ready, 16)
            for layer in range(LAYERS):
                first = layer * EXPERTS
                with sp.Fori(0, EXPERTS // 2 - 1) as it:
                    for slot in range(2):
                        sp.wait_ge(w_ready, it * 2 + (first + slot + 1))
                        load_expert(layer, it * 2 + (2 + slot), slot)
                if layer + 1 < LAYERS:
                    for slot in range(2):
                        sp.wait_ge(w_ready, first + EXPERTS - 2 + slot + 1)
                        load_expert(layer + 1, slot, slot)
            for g in range(GROUPS):
                sp.wait_ge(y_free, LAYERS * YPL - GROUPS + g + 1 + Y_BANKS)
                bs = slice(g * GROUP, (g + 1) * GROUP)
                sp.dma_start(out[bs].rearrange("b t d -> t b d"), X[:, bs, :]).then_inc(out_done, 16)
            sp.wait_ge(out_done, 16 * GROUPS)

        @block.gpsimd
        def _(pool):
            pool.dma_start(tau_raw[:, :], tau.partition_broadcast(P)).then_inc(in_small, 16)
            pool.dma_start(delta_raw[:, :], delta).then_inc(in_small, 16)
            for layer in range(LAYERS):
                pool.dma_start(bv_all[:, layer, :], bv[layer].partition_broadcast(P)).then_inc(in_small, 16)
                pool.dma_start(bo_all[:, layer, :], bo[layer].partition_broadcast(P)).then_inc(in_small, 16)
                pool.dma_start(wg_raw[:, layer, :], wg[layer]).then_inc(in_small, 16)
                pool.dma_start(b2_sb[:, layer, :], b2[layer]).then_inc(in_small, 16)
            pool.dma_start(bg_all[:, :], bg.partition_broadcast(P)).then_inc(in_small, 16)
            pool.memset(ident[:, :], 0.0).then_inc(pool_step, 1)
            pool.memset(lower[:, :, :], 1.0).then_inc(pool_step, 1)
            pool.wait_ge(pool_step, 2)
            pool.affine_select(out=ident[:, :], in_=ident[:, :], compare_op=ALU.not_equal, fill=1.0,
                               base=0, pattern=[[-1, P]], channel_multiplier=1).then_inc(const_ready, 1)
            pool.affine_select(out=lower[:, :, :], in_=lower[:, :, :], compare_op=ALU.is_gt, fill=0.0, base=0,
                               pattern=[[1, EXPERTS], [-1, EXPERTS]], channel_multiplier=0).then_inc(const_ready, 1)
            for sel in (sel_q_hi, sel_q_lo, sel_k_hi, sel_k_lo):
                pool.memset(f32(sel[:, :, :]), 0.0).then_inc(const_ready, 1)
            pool.memset(k_extra[:, :], 0.0).then_inc(const_ready, 1)
            pool.memset(minus_half[:, :], -0.5).then_inc(const_ready, 1)
            pool.memset(v_sb[:, :, :, :, :], 1.0).then_inc(const_ready, 1)
            pool.memset(max_cols[:, :, :], 0.0).then_inc(const_ready, 1)

            def split_expert(layer, e, slot, first_use):
                pool.wait_ge(w_load[slot], first_use)
                pool.sem_inc(pool_waits, 1)
                for raw, hi in ((w1_raw, w1_hi), (w2_raw, w2_hi)):
                    r, h = raw[:, slot], hi[:, slot]
                    pool.tensor_copy(h, r).then_inc(pool_step, 1)

            def split_expert_lo(slot):
                for raw, hi, lo, ready in ((w1_raw, w1_hi, w1_lo, None), (w2_raw, w2_hi, w2_lo, w_ready)):
                    ins = pool.tensor_tensor(lo[:, slot], raw[:, slot], f32(hi[:, slot]), ALU.subtract)
                    if ready is not None:
                        ins.then_inc(ready, 1)

            step = 2
            for slot in range(2):
                split_expert(0, slot, slot, 32)
                step += 2
                pool.wait_ge(pool_step, step)
                split_expert_lo(slot)
            for layer in range(LAYERS):
                for piece in ORDER[layer]:
                    kind, g = piece[0], piece[2]
                    if kind in ("ln1", "ln2"):
                        n = uses_before(layer, kind, g, kind == "ln2")
                        n = LN_INDEX[piece]
                        pool.wait_ge(var_ready, n + 1)
                        pool.tensor_tensor(rstd[:, :], var_eps[:, :], minus_half[:, :], ALU.pow).then_inc(rstd_ready, 1)
                        if kind == "ln1":
                            pool.wait_ge(xn_ready, n + 1)
                            if g == 0 and layer == 0:
                                pool.wait_ge(in_small, 16 * N_SMALL)
                            bs = slice(g * GROUP, (g + 1) * GROUP)
                            pool.tensor_tensor(X[:, bs, :], X[:, bs, :],
                                               bo_all[:, layer, :].unsqueeze(1).broadcast_to([P, GROUP, P]),
                                               ALU.add).then_inc(bo_added, 1)
                    if kind in ("kp", "qp"):
                        k = int(kind == "qp")
                        n = SPLIT_INDEX[piece]
                        if n >= 2:
                            last = ("qs" if k else "ks", *SPLITS[n - 2][1:], HG - 1)
                            wait_full(pool, MISC_USE[last])
                        pool.wait_ge(part_hi_ready, n + 1)
                        pool.tensor_tensor(part_lo[:, k, :], full[:, k, :], f32(part_hi[:, k, :]),
                                           ALU.subtract).then_inc(part_lo_ready, 1)
                def two_ahead(e, slot, loads, steps):
                    pool.wait_ge(y_full, (e + 1) * GROUPS + layer * YPL)
                    split_expert(layer, e, slot, loads)
                    pool.wait_ge(pool_step, steps)
                    split_expert_lo(slot)

                pairs = EXPERTS // 2
                with pool.Fori(0, pairs - 1) as it:
                    for slot in range(2):
                        two_ahead(it * 2 + slot, slot, (it + 2) * 32 + layer * pairs * 32,
                                  it * 4 + (step + 2 * slot + 2))
                step += 4 * (pairs - 1)
                if layer + 1 < LAYERS:
                    for slot in range(2):
                        step += 2
                        two_ahead(EXPERTS - 2 + slot, slot, (layer + 1) * pairs * 32 + 32, step)

        @block.tensor
        def _(pe):
            def claim(piece):
                b, n = misc(piece)
                if n >= MISC_BANKS:
                    pe.wait_ge(misc_done[n % MISC_BANKS], n // MISC_BANKS)
                return b

            def product(dst, hi, lo, rhi, rlo):
                pe.matmul(dst, hi, rhi, start=True, stop=False)
                pe.matmul(dst, hi, rlo, start=False, stop=False)
                return pe.matmul(dst, lo, rhi, start=False, stop=True)

            def tokens(b):
                return slice(b * P, (b + 1) * P)

            pe.wait_ge(const_ready, N_CONST)
            pe.wait_ge(in_w, 16 * 4 * LAYERS)
            for layer in range(LAYERS):
                dst = claim(("wT", layer))
                for k in range(4):
                    last = pe.transpose(dst[:, k * P:(k + 1) * P], w_raw[:, layer, k, :], ident[:, :])
                last.then_inc(misc_full, 1)
            pe.wait_ge(in_rows, 16 * 3 * LAYERS)
            dst = claim(("rT",))
            pe.transpose(dst[:, 0:N_ROWS], rows_raw[0:N_ROWS, :], ident[0:N_ROWS, 0:N_ROWS]).then_inc(misc_full, 1)

            for layer in range(LAYERS):
                if layer > 0:
                    pe.wait_ge(h_free, layer * HPL + H_BANKS)
                    pe.wait_ge(y_free, layer * YPL + Y_BANKS)
                for piece in ORDER[layer]:
                    kind = piece[0]
                    g = b = piece[2]
                    grp = slice(g * GT, (g + 1) * GT)
                    if kind == "ctxT":
                        pe.wait_ge(in_ctx[g], 16)
                        dst = claim(piece)
                        for t in range(GROUP):
                            last = pe.transpose(dst[:, tokens(t)], ctx_raw[:, g * GROUP + t, :], ident[:, :])
                        last.then_inc(misc_full, 1)
                    elif kind in ("xT1", "xT2"):
                        pe.wait_ge(xn_ready, LN_INDEX[("ln" + kind[2], layer, g)] + 1)
                        dst = claim(piece)
                        for t in range(GROUP):
                            last = pe.transpose(dst[:, tokens(t)], xn[:, t, :], ident[:, :])
                        last.then_inc(misc_full, 1)
                    elif kind == "kp":
                        wait_done(pe, ("wT", layer))
                        wait_done(pe, ("ctxT", 0, g))
                        dst = claim(piece)
                        product(dst[:, :], w_hi[:, layer, 1, :], w_lo[:, layer, 1, :],
                                ctx_hi[:, grp], ctx_lo[:, grp]).then_inc(misc_full, 1)
                    elif kind == "qp":
                        wait_done(pe, ("xT1", layer, g))
                        dst = claim(piece)
                        product(dst[:, :], w_hi[:, layer, 0, :], w_lo[:, layer, 0, :],
                                xt_hi[:, grp], xt_lo[:, grp]).then_inc(misc_full, 1)
                    elif kind == "vp":
                        dst = claim(piece)
                        for t in range(GROUP):
                            at = tokens(g * GROUP + t)
                            last = product(dst[:, tokens(t)], ctx_hi[:, at], ctx_lo[:, at],
                                           w_hi[:, layer, 2, :], w_lo[:, layer, 2, :])
                        last.then_inc(misc_full, 1)
                    elif kind in ("qs", "ks"):
                        j = piece[3]
                        k = int(kind == "qs")
                        if j == 0:
                            pe.wait_ge(part_lo_ready, SPLIT_INDEX[("qp" if k else "kp", layer, g)] + 1)
                            pe.wait_ge(sel_ready, 1)
                        dst = claim(piece)
                        hi, lo = (sel_q_hi, sel_q_lo) if k else (sel_k_hi, sel_k_lo)
                        pe.matmul(dst[:, :], hi[:, j, :], part_hi[:, k, :], start=True, stop=False)
                        pe.matmul(dst[:, :], lo[:, j, :], part_lo[:, k, :], start=False, stop=True).then_inc(misc_full, 1)
                    elif kind == "A":
                        i = piece[3]
                        n = layer * UPL + b * UNITS + i
                        grp_ = b // GROUP
                        if b % GROUP == 0 and i == 0:
                            for j in range(HG):
                                wait_done(pe, ("qs", layer, grp_, j))
                                wait_done(pe, ("ks", layer, grp_, j))
                        if n >= 2:
                            pe.wait_ge(a_free, n - 1)
                        rows = slice(HROWS * i, HROWS * (i + 1))
                        at = tokens(b % GROUP)
                        for j in range(HG):
                            last = pe.matmul(a_bank[n % 2][:, j * P:(j + 1) * P], q_tile(grp_)[rows, j, at],
                                             k_tile(grp_)[rows, j, at], start=True, stop=True)
                        last.then_inc(a_full, 1)
                    elif kind == "mT":
                        pe.wait_ge(max_ready, layer * BATCHES + b + 1)
                        dst = claim(piece)
                        for j in range(HG):
                            last = pe.transpose(dst[:, j * P:(j + 1) * P], max_cols[:, j, :], ident[:, :])
                        last.then_inc(misc_full, 1)
                    elif kind == "B":
                        i = piece[3]
                        n = layer * UPL + b * UNITS + i
                        if i == 0:
                            wait_done(pe, ("mT", layer, b))
                        if n >= 2:
                            pe.wait_ge(b_free, n - 1)
                        rows = slice(HROWS * i, HROWS * (i + 1))
                        at = tokens(b % GROUP)
                        for j in range(HG):
                            last = pe.matmul(b_bank[n % 2][:, j * P:(j + 1) * P], k_tile(b // GROUP)[rows, j, at],
                                             q2[rows, b % 2, j, :], start=True, stop=True)
                        last.then_inc(b_full, 1)
                    elif kind == "PV":
                        i = piece[3]
                        n = layer * UPL + b * UNITS + i
                        pe.wait_ge(b_free, n + 1)
                        if i == 0:
                            if b % GROUP == 0:
                                wait_done(pe, ("vp", layer, b // GROUP))
                            pe.wait_ge(pv_free, layer * BATCHES + b)
                        for j in range(HG):
                            h = HG * j + i
                            last = pe.matmul(pv_bank[:, h * 16:h * 16 + HD + 1], probs[:, b % 2, i, j, :],
                                             v_sb[:, (b // GROUP) % 2, b % GROUP, h, :], start=True, stop=True)
                        if i == UNITS - 1:
                            last.then_inc(pv_full, 1)
                    elif kind == "oT":
                        pe.wait_ge(attn_ready, layer * BATCHES + b + 1)
                        dst = claim(piece)
                        pe.transpose(dst[:, 0:P], attn[:, :], ident[:, :]).then_inc(misc_full, 1)
                    elif kind == "wo":
                        wait_done(pe, ("oT", layer, b))
                        dst = claim(piece)
                        product(dst[:, 0:P], attn_hi[:, b % 2, :], attn_lo[:, b % 2, :],
                                w_hi[:, layer, 3, :], w_lo[:, layer, 3, :]).then_inc(misc_full, 1)
                    elif kind == "lg":
                        wait_done(pe, ("xT2", layer, g))
                        dst = claim(piece)
                        for t in range(GROUP):
                            at = tokens(g * GROUP + t)
                            last = product(dst[:, t * EXPERTS:(t + 1) * EXPERTS], xt_hi[:, at], xt_lo[:, at],
                                           wg_hi[:, layer, :], wg_lo[:, layer, :])
                        last.then_inc(misc_full, 1)
                    elif kind == "gT":
                        pe.wait_ge(gates_ready, layer * GROUPS + g + 1)
                        dst = claim(piece)
                        for t in range(GROUP):
                            last = pe.transpose(dst[0:EXPERTS, tokens(t)], gates[:, :, g * GROUP + t], ident[:, :])
                        last.then_inc(misc_full, 1)
                    elif kind == "b2":
                        wait_done(pe, ("gT", layer, g))
                        dst = claim(piece)
                        for t in range(GROUP):
                            last = pe.matmul(dst[:, tokens(t)], gates_t[:, tokens(t)], b2_sb[:, layer, :],
                                             start=True, stop=True)
                        last.then_inc(misc_full, 1)

                pe.wait_ge(a_free, (layer + 1) * UPL)
                pe.wait_ge(b_free, (layer + 1) * UPL)
                pe.wait_ge(pv_free, (layer + 1) * BATCHES)
                last_use = MISC_USE[("b2", layer, GROUPS - 1)]
                for n in range(last_use - MISC_BANKS + 1, last_use + 1):
                    pe.wait_ge(misc_done[n % MISC_BANKS], n // MISC_BANKS + 1)

                def hidden_chunk(it, slot, g, c):
                    n = (slot * GROUPS + g) * FC + c
                    if g == 0 and c == 0:
                        pe.wait_ge(w_ready, it * 2 + (layer * EXPERTS + slot + 1))
                    pe.wait_ge(h_free, it * (2 * GROUPS * FC) + (layer * HPL + n + 1))
                    dst = h_bank[c % H_BANKS][:, :]
                    cs, ts = slice(c * P, (c + 1) * P), slice(g * GT, (g + 1) * GT)
                    product(dst, w1_hi[:, slot, cs], w1_lo[:, slot, cs], xt_hi[:, ts], xt_lo[:, ts]).then_inc(h_full, 1)

                def output_block(it, slot, g, t):
                    u = slot * GROUPS + g
                    if t == 0:
                        pe.wait_ge(hl_ready, it * (2 * GROUPS * FC) + (layer * HPL + (u + 1) * FC + 2))
                        pe.wait_ge(y_free, it * (2 * GROUPS) + (layer * YPL + u + 1))
                    dst = y_bank[u % 2][:, tokens(t)]
                    hi, lo = hidden_part(0, u % 2), hidden_part(1, u % 2)
                    k = 0
                    for c in range(FC):
                        for a, w in ((hi, w2_hi), (hi, w2_lo), (lo, w2_hi)):
                            last = pe.matmul(dst, a[:, c, tokens(t)], w[:, slot, c, :], start=(k == 0), stop=(k == 3 * FC - 1))
                            k += 1
                    if t == GROUP - 1:
                        last.then_inc(y_full, 1)

                def expert_pair(it, last_pair):
                    units = [(it, slot, g) for slot in range(2) for g in range(GROUPS)]
                    follow = units[1:] + ([] if last_pair else [(it + 1, 0, 0)])
                    for k, unit in enumerate(units):
                        for c in range(FC):
                            if k < len(follow):
                                hidden_chunk(*follow[k], c)
                            output_block(*unit, c)

                for c in range(FC):
                    hidden_chunk(0, 0, 0, c)
                with pe.Fori(0, EXPERTS // 2 - 1) as it:
                    expert_pair(it, False)
                expert_pair(EXPERTS // 2 - 1, True)

        @block.scalar
        def _(act):
            act.sem_inc(h_free, H_BANKS)
            hi_target = {"wT": lambda p: w_hi[:, p[1], :, :].rearrange("p k n -> p (k n)"),
                         "ctxT": lambda p: ctx_hi[:, p[2] * GT:(p[2] + 1) * GT],
                         "xT1": lambda p: xt_hi[:, p[2] * GT:(p[2] + 1) * GT],
                         "xT2": lambda p: xt_hi[:, p[2] * GT:(p[2] + 1) * GT],
                         "oT": lambda p: attn_hi[:, p[2] % 2, :]}

            def hi_part(piece):
                src, n = misc(piece)
                wait_full(act, n)
                dst = hi_target[piece[0]](piece)
                act.activation(dst, src[:, 0:dst.shape[1]], ACT.Copy).then_inc(hi_ready, 1)

            for layer in range(LAYERS):
                hi_part(("wT", layer))
            src, n = misc(("rT",))
            wait_full(act, n)
            act.activation(cols[:, 0:N_ROWS], src[:, 0:N_ROWS], ACT.Copy).then_inc(done(n), 1)
            for layer in range(LAYERS):
                for piece in ORDER[layer]:
                    kind = piece[0]
                    g = b = piece[2]
                    if kind in hi_target:
                        hi_part(piece)
                    elif kind in ("kp", "qp"):
                        k = int(kind == "qp")
                        n = SPLIT_INDEX[piece]
                        if n >= 2:
                            wait_full(act, MISC_USE[("qs" if k else "ks", *SPLITS[n - 2][1:], HG - 1)])
                        act.wait_ge(full_ready, n + 1)
                        act.activation(part_hi[:, k, :], full[:, k, :], ACT.Copy).then_inc(part_hi_ready, 1)
                    elif kind == "qs":
                        src, n = misc(piece)
                        wait_full(act, n)
                        if piece[3] == 0:
                            act.wait_ge(sel_ready, 1)
                        act.activation(q_tile(g)[:, piece[3], :], src[:, :], ACT.Identity,
                                       bias=one_cols[:, 0:1]).then_inc(done(n), 1)
                    elif kind == "B":
                        i = piece[3]
                        n = layer * UPL + b * UNITS + i
                        act.wait_ge(b_full, n + 1)
                        if i == 0 and layer * BATCHES + b >= 2:
                            act.wait_ge(pv_full, layer * BATCHES + b - 1)
                        act.activation(probs[:, b % 2, i, :, :].rearrange("p j l -> p (j l)"), b_bank[n % 2][:, :],
                                       ACT.Exp).then_inc(b_free, 1)
                    elif kind == "lg":
                        act.wait_ge(shifted_ready, layer * GROUPS + g + 1)
                        act.activation(expd[:, :, :], shifted[:, :, :], ACT.Exp).then_inc(exp_ready, 1)
                    elif kind == "gT":
                        src, n = misc(piece)
                        wait_full(act, n)
                        act.activation(gates_t[:, :], src[0:EXPERTS, :], ACT.Copy).then_inc(done(n), 1)

                func = (ACT.Relu, ACT.Gelu)[layer]

                def expert_pair(it):
                    for slot in range(2):
                        for g in range(GROUPS):
                            for c in range(FC):
                                n = (slot * GROUPS + g) * FC + c
                                per = 2 * GROUPS * FC
                                act.wait_ge(h_full, it * per + (layer * HPL + n + 1))
                                act.wait_ge(hl_ready, it * per + (layer * HPL + n + 1))
                                act.sem_inc(act_step, 1)
                                col = it * (2 * FC) + (layer * B1_ROWS + slot * FC + c)
                                act.activation(hidden[:, c % 2, :], h_bank[c % H_BANKS][:, :], func,
                                               bias=cols[:, bass.ds(col, 1)]).then_inc(h_free, 1)

                with act.Fori(0, EXPERTS // 2) as it:
                    expert_pair(it)

        @block.vector
        def _(dve):
            steps = [0]

            def chained(ins):
                steps[0] += 1
                ins.then_inc(dve_step, 1)
                dve.wait_ge(dve_step, steps[0])

            dve.sem_inc(hl_ready, 2)
            dve.sem_inc(y_free, Y_BANKS)
            hi_count = [0]
            split_target = {"wT": lambda p: (w_hi[:, p[1], :, :].rearrange("p k n -> p (k n)"), w_lo[:, p[1], :, :].rearrange("p k n -> p (k n)")),
                            "ctxT": lambda p: tuple(a[:, p[2] * GT:(p[2] + 1) * GT] for a in (ctx_hi, ctx_lo)),
                            "xT1": lambda p: tuple(a[:, p[2] * GT:(p[2] + 1) * GT] for a in (xt_hi, xt_lo)),
                            "xT2": lambda p: tuple(a[:, p[2] * GT:(p[2] + 1) * GT] for a in (xt_hi, xt_lo)),
                            "oT": lambda p: tuple(a[:, p[2] % 2, :] for a in (attn_hi, attn_lo))}

            def lo_part(piece):
                src, n = misc(piece)
                hi, lo = split_target[piece[0]](piece)
                hi_count[0] += 1
                dve.wait_ge(hi_ready, hi_count[0])
                dve.tensor_tensor(lo, src[:, 0:hi.shape[1]], f32(hi), ALU.subtract).then_inc(done(n), 1)

            dve.wait_ge(const_ready, N_CONST)
            heads = ident[:, :].rearrange("p (j i e) -> p j i e", j=HG, i=HG)
            for sel, octets in ((sel_q_hi, (0, 1)), (sel_q_lo, (2,)), (sel_k_hi, (0, 2)), (sel_k_lo, (1,))):
                for r in octets:
                    dve.tensor_copy(sel[:, :, :].rearrange("p j (i r e) -> p j i r e", i=HG, e=HD)[:, :, :, r, :],
                                    heads)
            by_row = ident[:, :].rearrange("p (i r) -> p r i", r=HROWS)
            for k, row in enumerate((ROW_ONE, ROW_MAX)):
                dve.tensor_reduce(one_cols[:, k:k + 1], by_row[:, row:row + 2, :], AX.XY, ALU.add)
            dve.wait_ge(in_small, 16 * N_SMALL)
            dve.tensor_copy(wg_hi[:, :, :], wg_raw[:, :, :])
            dve.tensor_scalar(tau_sc[:, :], tau_raw[:, :], SOFTMAX_SCALE, None, ALU.mult)
            chained(dve.tensor_scalar(delta_sc[:, :], delta_raw[:, :], SOFTMAX_SCALE, None, ALU.mult))
            dve.tensor_tensor(wg_lo[:, :, :], wg_raw[:, :, :], f32(wg_hi[:, :, :]), ALU.subtract).then_inc(sel_ready, 1)
            chained(dve.tensor_copy(delta_hi[:, :], delta_sc[:, :]))
            dve.tensor_tensor(delta_lo[:, :], delta_sc[:, :], f32(delta_hi[:, :]), ALU.subtract).then_inc(delta_ready, 1)
            dve.tensor_scalar(k_extra[:, :], k_extra[:, :], one_cols[:, 1:2], None, ALU.add).then_inc(delta_ready, 1)
            for layer in range(LAYERS):
                lo_part(("wT", layer))
            wait_done(dve, ("rT",))

            by_head = max_cols[:, :, :].rearrange("p j (i r) -> p i j r", r=HROWS)
            for layer in range(LAYERS):
                for piece in ORDER[layer]:
                    kind = piece[0]
                    g = b = piece[2]
                    bs = slice(g * GROUP, (g + 1) * GROUP)
                    if kind in ("ln1", "ln2"):
                        n = LN_INDEX[piece]
                        if kind == "ln1" and layer == 0:
                            dve.wait_ge(in_x[g], 16)
                        if n:
                            wait_full(dve, MISC_USE[("xT" + LNS[n - 1][0][2], *LNS[n - 1][1:])])
                        for t in range(GROUP):
                            ins = dve.bn_stats(stats[:, t, :], X[:, g * GROUP + t, :])
                        chained(ins)
                        for t in range(GROUP):
                            ins = dve.bn_aggr(mv[:, t, :], stats[:, t, :])
                        chained(ins)
                        dve.tensor_scalar(var_eps[:, :], mv[:, :, 1], LN_EPS, None, ALU.add).then_inc(var_ready, 1)
                        dve.wait_ge(rstd_ready, n + 1)
                        for t in range(GROUP):
                            ins = dve.tensor_scalar(xn[:, t, :], X[:, g * GROUP + t, :], mv[:, t, 0:1],
                                                    rstd[:, t:t + 1], ALU.subtract, ALU.mult)
                        ins.then_inc(xn_ready, 1)
                    elif kind in split_target:
                        lo_part(piece)
                    elif kind in ("kp", "qp"):
                        k = int(kind == "qp")
                        src, n = misc(piece)
                        m = SPLIT_INDEX[piece]
                        if m >= 2:
                            dve.wait_ge(part_lo_ready, m - 1)
                        wait_full(dve, n)
                        bias = LAYERS * B1_ROWS + 2 * layer + (1 - k)
                        if k:
                            ins = dve.scalar_tensor_tensor(
                                out=full[:, 1, :].rearrange("p (b t) -> p b t", t=P),
                                in0=src[:, :].rearrange("p (b t) -> p b t", t=P), scalar=cols[:, bias:bias + 1],
                                in1=tau_sc[:, bs].unsqueeze(2).broadcast_to([P, GROUP, P]), op0=ALU.add, op1=ALU.mult)
                        else:
                            ins = dve.tensor_scalar(full[:, 0, :], src[:, :], cols[:, bias:bias + 1], None, ALU.add)
                        steps[0] += 1
                        ins.then_inc(dve_step, 1)
                        dve.wait_ge(dve_step, steps[0])
                        dve.sem_inc(full_ready, 1)
                        dve.sem_inc(done(n), 1)
                    elif kind == "vp":
                        src, n = misc(piece)
                        wait_full(dve, n)
                        for t in range(GROUP):
                            ins = dve.tensor_tensor(
                                v_sb[:, g % 2, t, :, 0:HD], src[:, t * P:(t + 1) * P].rearrange("p (h e) -> p h e", e=HD),
                                bv_all[:, layer, :].rearrange("p (h e) -> p h e", e=HD), ALU.add)
                        ins.then_inc(done(n), 1)
                    elif kind == "ks":
                        src, n = misc(piece)
                        wait_full(dve, n)
                        if layer == 0 and g == 0:
                            dve.wait_ge(extra_ready, 16 * 2 * HG)
                        dve.tensor_tensor(k_tile(g)[:, piece[3], :], src[:, :], k_extra[:, g * GT:(g + 1) * GT],
                                          ALU.add).then_inc(done(n), 1)
                    elif kind == "A":
                        i = piece[3]
                        n = layer * UPL + b * UNITS + i
                        dve.wait_ge(a_full, n + 1)
                        dve.tensor_reduce(neg_max[:, i * HG:(i + 1) * HG],
                                          a_bank[n % 2][:, :].rearrange("p (j s) -> p j s", s=P),
                                          AX.X, ALU.max, negate=True).then_inc(a_free, 1)
                        if i == UNITS - 1:
                            dve.wait_ge(a_free, n + 1)
                            m = neg_max[:, :].rearrange("p (i j) -> p i j", j=HG)
                            chained(dve.tensor_copy(by_head[:, :, :, ROW_MAX].bitcast(F32R), m))
                            dve.tensor_tensor(by_head[:, :, :, ROW_MAX + 1], m, by_head[:, :, :, ROW_MAX],
                                              ALU.subtract).then_inc(max_ready, 1)
                    elif kind == "mT":
                        src, n = misc(piece)
                        wait_full(dve, n)
                        at = slice((b % GROUP) * P, (b % GROUP + 1) * P)
                        dve.tensor_tensor(q2[:, b % 2, :, :], src[:, :].rearrange("p (j l) -> p j l", l=P),
                                          f32(q_tile(b // GROUP)[:, :, at]), ALU.add).then_inc(done(n), 1)
                    elif kind == "PV" and piece[3] == UNITS - 1:
                        dve.wait_ge(pv_full, layer * BATCHES + b + 1)
                        pv = pv_bank[:, 0:HEADS * 16].rearrange("p (h e) -> p h e", e=16)
                        chained(dve.reciprocal(rec[:, :], pv[:, :, HD]))
                        steps[0] += 1
                        dve.tensor_tensor(attn[:, :].rearrange("p (h e) -> p h e", e=HD), pv[:, :, 0:HD],
                                          rec[:, :].unsqueeze(2).broadcast_to([P, HEADS, HD]), ALU.mult)\
                            .then_inc(dve_step, 1)
                        dve.wait_ge(dve_step, steps[0])
                        dve.sem_inc(attn_ready, 1)
                        dve.sem_inc(pv_free, 1)
                    elif kind == "wo":
                        src, n = misc(piece)
                        wait_full(dve, n)
                        if b % GROUP == 0:
                            dve.wait_ge(bo_added, layer * GROUPS + b // GROUP + 1)
                        dve.tensor_tensor(X[:, b, :], src[:, 0:P], X[:, b, :], ALU.add).then_inc(done(n), 1)
                        if b % GROUP == GROUP - 1:
                            wait_done(dve, piece)
                    elif kind == "lg":
                        src, n = misc(piece)
                        wait_full(dve, n)
                        logit_src = src[:, 0:GROUP * EXPERTS].rearrange("p (b e) -> p b e", e=EXPERTS)
                        if layer == 1:
                            ins = dve.tensor_tensor(logits[:, :, :], logit_src,
                                                    bg_all[:, :].unsqueeze(1).broadcast_to([P, GROUP, EXPERTS]), ALU.add)
                        else:
                            ins = dve.tensor_copy(logits[:, :, :], logit_src)
                        ins.then_inc(done(n), 1)
                        wait_done(dve, piece)
                        top, total, rtotal, picked, guarded, rpicked = (gsmall[:, k, :] for k in range(6))

                        def over_experts(a):
                            return a.unsqueeze(2).broadcast_to([P, GROUP, EXPERTS])

                        chained(dve.tensor_reduce(top, logits[:, :, :], AX.X, ALU.max))
                        dve.tensor_tensor(shifted[:, :, :], logits[:, :, :], over_experts(top), ALU.subtract)\
                           .then_inc(shifted_ready, 1)
                        other = logits[:, :, :].unsqueeze(2).broadcast_to([P, GROUP, EXPERTS, EXPERTS])
                        own = logits[:, :, :].unsqueeze(3).broadcast_to([P, GROUP, EXPERTS, EXPERTS])
                        dve.tensor_tensor(cmp_gt[:, :, :, :], other, own, ALU.is_gt)
                        chained(dve.tensor_tensor(cmp_eq[:, :, :, :], other, own, ALU.is_equal))
                        low = lower[:, :, :].rearrange("p a c -> p (a c)").unsqueeze(1).broadcast_to([P, GROUP, EXPERTS * EXPERTS])
                        flat = "p b a c -> p b (a c)"
                        chained(dve.tensor_tensor(cmp_eq[:, :, :, :].rearrange(flat), cmp_eq[:, :, :, :].rearrange(flat), low, ALU.mult))
                        chained(dve.tensor_tensor(cmp_gt[:, :, :, :], cmp_gt[:, :, :, :], cmp_eq[:, :, :, :], ALU.add))
                        dve.tensor_reduce(rank[:, :, :], cmp_gt[:, :, :, :], AX.X, ALU.add)
                        dve.wait_ge(exp_ready, layer * GROUPS + g + 1)
                        weight = expd
                        if layer == 1:
                            chained(dve.tensor_reduce(total, expd[:, :, :], AX.X, ALU.add))
                            chained(dve.reciprocal(rtotal, total))
                            chained(dve.tensor_tensor(shifted[:, :, :], expd[:, :, :], over_experts(rtotal), ALU.mult))
                            weight = shifted
                        else:
                            chained(dve.tensor_copy(total, top))
                        chained(dve.scalar_tensor_tensor(out=numer[:, :, :], in0=rank[:, :, :], scalar=1.5,
                                                         in1=weight[:, :, :], op0=ALU.is_lt, op1=ALU.mult))
                        chained(dve.tensor_reduce(picked, numer[:, :, :], AX.X, ALU.add))
                        chained(dve.tensor_scalar(guarded, picked, GATE_EPS, None, ALU.max))
                        chained(dve.reciprocal(rpicked, guarded))
                        dve.tensor_tensor(gates[:, :, bs].rearrange("p e b -> p b e"), numer[:, :, :],
                                          over_experts(rpicked), ALU.mult).then_inc(gates_ready, 1)
                    elif kind == "b2":
                        src, n = misc(piece)
                        wait_full(dve, n)
                        dve.tensor_tensor(X[:, bs, :], src[:, :].rearrange("p (b d) -> p b d", d=P), X[:, bs, :],
                                          ALU.add).then_inc(done(n), 1)
                        wait_done(dve, piece)

                per = 2 * GROUPS

                def split_hidden(it, slot, g):
                    u = slot * GROUPS + g
                    for c in range(FC):
                        n = layer * HPL + u * FC + c
                        dve.wait_ge(h_free, it * (per * FC) + (n + 1 + H_BANKS))
                        dve.tensor_copy(hidden_part(0, u % 2)[:, c, :], hidden[:, c % 2, :]).then_inc(hh_ready, 1)
                        dve.wait_ge(hh_ready, it * (per * FC) + (n + 1))
                        dve.tensor_tensor(hidden_part(1, u % 2)[:, c, :], hidden[:, c % 2, :],
                                          f32(hidden_part(0, u % 2)[:, c, :]), ALU.subtract).then_inc(hl_ready, 1)

                def add_output(it, slot, g):
                    u = slot * GROUPS + g
                    dve.wait_ge(y_full, it * per + (layer * YPL + u + 1))
                    for t in range(GROUP):
                        b = g * GROUP + t
                        ins = dve.scalar_tensor_tensor(
                            out=X[:, b, :], in0=y_bank[u % 2][:, t * P:(t + 1) * P],
                            scalar=gates[:, bass.ds(it * 2 + slot, 1), b], in1=X[:, b, :], op0=ALU.mult, op1=ALU.add)
                    ins.then_inc(y_free, 1)

                def expert_pair(it, last_pair):
                    units = [(it, slot, g) for slot in range(2) for g in range(GROUPS)]
                    follow = units[1:] + ([] if last_pair else [(it + 1, 0, 0)])
                    for k, unit in enumerate(units):
                        if k < len(follow):
                            split_hidden(*follow[k])
                        add_output(*unit)

                split_hidden(0, 0, 0)
                with dve.Fori(0, EXPERTS // 2 - 1) as it:
                    expert_pair(it, False)
                expert_pair(EXPERTS // 2 - 1, True)
                dve.wait_ge(y_free, (layer + 1) * YPL + Y_BANKS)


LNS = [p for order in ORDER for p in order if p[0] in ("ln1", "ln2")]
LN_INDEX = {p: n for n, p in enumerate(LNS)}
SPLITS = [p for order in ORDER for p in order if p[0] in ("kp", "qp")]
SPLIT_INDEX = {p: n for n, p in enumerate(SPLITS)}
N_SMALL = 2 + 4 * LAYERS + 1
N_CONST = 10


def kernel(**inputs):
    import concourse.bacc as bacc
    from concourse.bass_utils import run_bass_kernel_spmd

    nc = bacc.Bacc("TRN2", target_bir_lowering=False, num_devices=1)
    arrays, aps = {}, {}
    for name, value in inputs.items():
        a = np.ascontiguousarray(value)
        arrays[f"in_{name}"] = a
        aps[name] = nc.dram_tensor(f"in_{name}", a.shape, mybir.dt.from_np(a.dtype), kind="ExternalInput").ap()
    out = nc.dram_tensor("out_x", (BATCHES, P, P), F32, kind="ExternalOutput").ap()

    def both(part, names):
        return [[aps[f"L{layer}_{part}_{n}"] for n in names] for layer in range(LAYERS)]

    def each(name):
        return [aps[f"L{layer}_{name}"] for layer in range(LAYERS)]

    build(nc, aps["x"], aps["ctx_1024"], aps["condB_tau"], aps["fside_BxS2_0"],
          both("xcond", ("Wq", "Wk", "Wv", "Wo")), each("ffn_b1"), both("xcond", ("bq", "bk")),
          each("xcond_bv"), each("xcond_bo"), each("ffn_Wg"), aps["L1_ffn_bg"], each("ffn_W1"), each("ffn_W2"),
          each("ffn_b2"), out)
    r = run_bass_kernel_spmd(nc, [arrays], core_ids=[0])
    return r.results[0]["out_x"]
```

```python
from contextlib import ExitStack

import numpy as np

import concourse.bass as bass
from concourse import mybir

F32 = mybir.dt.float32
F32R = mybir.dt.float32r
ALU = mybir.AluOpType
ACT = mybir.ActivationFunctionType
AX = mybir.AxisListType

P = 128
LAYERS = 2
BATCHES = 16
GROUP = 4
GROUPS = BATCHES // GROUP
GT = GROUP * P
TOKENS = BATCHES * P
HEADS = 16
HD = P // HEADS
HG = 4
HROWS = P // HG
UNITS = HG
EXPERTS = 8
FF = 512
FC = FF // P
LN_EPS = 1e-5
GATE_EPS = 1e-12
SOFTMAX_SCALE = 1.0 / float(np.sqrt(HD))
MISC_BANKS = 3
H_BANKS = 2
VW = 16
HW = 32
Y_BANKS = 2
ROW_ONE, ROW_MAX = 3 * HD, 3 * HD + 2
B1_ROWS = EXPERTS * FC
MISC = ("wT", "rT", "ctxT", "xT1", "qp", "kp", "vp", "qs", "ks", "mT", "pT", "oT", "wo", "xT2", "lg", "gT",
        "b2", "acc")


def attention_order(layer):
    def prepare(g):
        first = [("ctxT", layer, g)] if layer == 0 else []
        return [first + [("xT1", layer, g), ("kp", layer, g)],
                [("qp", layer, g), ("vp", layer, g), ("ks", layer, g, 0), ("ks", layer, g, 1)],
                [("ks", layer, g, 2), ("ks", layer, g, 3)] + [("qs", layer, g, j) for j in range(HG)]]

    yield ("ln1", layer, 0)
    for part in prepare(0):
        yield from part
    for i in range(UNITS):
        yield ("A", layer, 0, i)
    yield ("mT", layer, 0)
    yield ("ln1", layer, 1)
    for s in range(BATCHES + 5):
        for i in range(UNITS):
            if s + 1 < BATCHES:
                yield ("A", layer, s + 1, i)
            if s < BATCHES:
                yield ("B", layer, s, i)
            if 1 <= s <= BATCHES:
                yield ("PV", layer, s - 1, i)
        if 2 <= s < BATCHES + 2:
            yield ("oT", layer, s - 2)
        g, r = s // GROUP + 1, s % GROUP
        if g < GROUPS and r < 3:
            yield from prepare(g)[r]
        if s + 1 < BATCHES:
            yield ("mT", layer, s + 1)
        if 2 <= s < BATCHES + 2:
            yield ("wo", layer, s - 2)
        if 1 <= s <= BATCHES:
            yield ("pT", layer, s - 1)
        if g + 1 < GROUPS and r == 3:
            yield ("ln1", layer, g + 1)
        for name, at in (("ln2", 5), ("xT2", 6), ("lg", 7), ("gT", 8), ("b2", 8)):
            if s >= at and (s - at) % GROUP == 0 and (s - at) // GROUP < GROUPS:
                yield (name, layer, (s - at) // GROUP)


ORDER = [list(attention_order(layer)) for layer in range(LAYERS)]
USES = [("wT", layer) for layer in range(LAYERS)] + [("rT",)]
for layer_, order_ in enumerate(ORDER):
    USES += [p for p in order_ if p[0] in MISC] + [("acc", layer_, g_) for g_ in range(GROUPS)]
MISC_USE = {piece: n for n, piece in enumerate(USES)}


def build(nc, x, ctx_in, tau, delta, wts, b1, bqk, bv, bo, wg, bg, w1, w2, b2, out):
    stack = ExitStack()
    with stack:
        def sb(name, shape, dt=F32):
            return stack.enter_context(nc.sbuf_tensor(name, shape, dt))

        def sem(name):
            return stack.enter_context(nc.semaphore(name))

        def f32(ap):
            return ap.bitcast(F32)

        X = sb("X", [P, BATCHES, P])
        ctx_raw = sb("ctx_raw", [P, BATCHES, P])
        ctx_hi, ctx_lo = sb("ctx_hi", [P, TOKENS], F32R), sb("ctx_lo", [P, TOKENS], F32R)
        xt_hi, xt_lo = sb("xt_hi", [P, TOKENS], F32R), sb("xt_lo", [P, TOKENS], F32R)
        w_raw = sb("w_raw", [P, LAYERS, 4, P])
        w_hi, w_lo = sb("w_hi", [P, LAYERS, 4, P], F32R), sb("w_lo", [P, LAYERS, 4, P], F32R)
        rows_raw = sb("rows_raw", [P, P])
        cols = sb("cols", [P, P])
        N_ROWS = LAYERS * (B1_ROWS + 2)
        ident = sb("ident", [P, P])
        one_cols = sb("one_cols", [P, 2])
        sel_q_hi, sel_q_lo = sb("sel_q_hi", [P, HG, P], F32R), sb("sel_q_lo", [P, HG, P], F32R)
        sel_k_hi, sel_k_lo = sb("sel_k_hi", [P, HG, P], F32R), sb("sel_k_lo", [P, HG, P], F32R)
        tau_sc = sb("tau_sc", [P, BATCHES])
        tau_raw = sb("tau_raw", [P, BATCHES])
        delta_raw = sb("delta_raw", [BATCHES, P])
        delta_sc = sb("delta_sc", [BATCHES, P])
        delta_hi, delta_lo = sb("delta_hi", [BATCHES, P], F32R), sb("delta_lo", [BATCHES, P])
        k_extra = sb("k_extra", [P, TOKENS])
        bv_all, bo_all = sb("bv_all", [P, LAYERS, P]), sb("bo_all", [P, LAYERS, P])
        wg_raw = sb("wg_raw", [P, LAYERS, EXPERTS])
        wg_hi, wg_lo = sb("wg_hi", [P, LAYERS, EXPERTS], F32R), sb("wg_lo", [P, LAYERS, EXPERTS], F32R)
        bg_all = sb("bg_all", [P, EXPERTS])
        b2_sb = sb("b2_sb", [2 * EXPERTS, LAYERS, P])
        lower = sb("lower", [P, EXPERTS, EXPERTS])
        stats, mv = sb("stats", [P, GROUP, 6]), sb("mv", [P, GROUP, 2])
        var_eps, rstd = sb("var_eps", [P, GROUP]), sb("rstd", [P, GROUP])
        minus_half = sb("minus_half", [P, GROUP])
        xn = sb("xn", [P, GROUP, P])
        full = sb("full", [P, 2, GT])
        part_hi, part_lo = sb("part_hi", [P, 2, GT], F32R), sb("part_lo", [P, 2, GT], F32R)
        big = sb("big", [P, 2, 2, HG, GT], F32R)
        q2 = sb("q2", [P, 2, HG, P], F32R)
        probs = sb("probs", [P, 2, UNITS, HG, P])
        v_sb = sb("v_sb", [P, 2, GROUP, HEADS, VW])
        heads_t = sb("heads_t", [P, HG * P])
        neg_max = sb("neg_max", [P, HEADS])
        max_cols = sb("max_cols", [P, HG, P])
        rec = sb("rec", [P, HEADS])
        attn = sb("attn", [P, P])
        attn_hi, attn_lo = sb("attn_hi", [P, 2, P], F32R), sb("attn_lo", [P, 2, P], F32R)
        logits, shifted = sb("logits", [P, GROUP, EXPERTS]), sb("shifted", [P, GROUP, EXPERTS])
        expd, numer = sb("expd", [P, GROUP, EXPERTS]), sb("numer", [P, GROUP, EXPERTS])
        gsmall = sb("gsmall", [P, 6, GROUP])
        cmp_gt, cmp_eq = (sb(n, [P, GROUP, EXPERTS, EXPERTS]) for n in ("cmp_gt", "cmp_eq"))
        rank = sb("rank", [P, GROUP, EXPERTS])
        gates_full = sb("gates_full", [P, GROUP, EXPERTS])
        gates = sb("gates", [P, 2, EXPERTS, BATCHES])
        gates_t = sb("gates_t", [2 * EXPERTS, TOKENS], F32R)
        gate_rows = sb("gate_rows", [2 * EXPERTS, 2, GT], F32R)
        ones = sb("ones", [2 * EXPERTS, P], F32R)
        own_rows = sb("own_rows", [2 * EXPERTS, EXPERTS])
        hidden = probs[:, 0, 0:2, :, :].rearrange("p s j l -> p s (j l)")
        gate_all = probs[:, 1, 0:2, :, :].rearrange("p s j l -> p s (j l)")
        weighted = full
        acc = ctx_raw[:, :, :].rearrange("p b d -> p (b d)")
        w1_raw, w2_raw = sb("w1_raw", [P, 2, FF]), sb("w2_raw", [P, 2, FC, P])
        w1_hi, w1_lo = sb("w1_hi", [P, 2, FF], F32R), sb("w1_lo", [P, 2, FF], F32R)
        w2_hi, w2_lo = sb("w2_hi", [P, 2, FC, P], F32R), sb("w2_lo", [P, 2, FC, P], F32R)

        bank = [stack.enter_context(nc.psum_tensor(f"bank{n}", [P, 512], F32)) for n in range(8)]
        a_bank, b_bank, pv_bank, misc_bank = bank[0:2], bank[2:4], bank[4], bank[5:8]
        h_bank, y_bank, gate_bank = bank[0:2], bank[2:4], bank[4]

        in_small, in_w = sem("in_small"), sem("in_w")
        in_x = [sem(f"in_x{g}") for g in range(GROUPS)]
        in_ctx = [sem(f"in_ctx{g}") for g in range(GROUPS)]
        in_rows, out_done = sem("in_rows"), sem("out_done")
        const_ready = sem("const_ready")
        sel_ready = sem("sel_ready")
        delta_ready, extra_ready = sem("delta_ready"), sem("extra_ready")
        misc_full = sem("misc_full")
        misc_done = [sem(f"misc_done{n}") for n in range(MISC_BANKS)]
        hi_ready = sem("hi_ready")
        var_ready, rstd_ready = sem("var_ready"), sem("rstd_ready")
        xn_ready, bo_added = sem("xn_ready"), sem("bo_added")
        full_ready, part_hi_ready, part_lo_ready = sem("full_ready"), sem("part_hi_ready"), sem("part_lo_ready")
        a_full, a_free, b_full, b_free = sem("a_full"), sem("a_free"), sem("b_full"), sem("b_free")
        max_ready = sem("max_ready")
        pv_full, pv_free, attn_ready = sem("pv_full"), sem("pv_free"), sem("attn_ready")
        shifted_ready, exp_ready, gates_ready = sem("shifted_ready"), sem("exp_ready"), sem("gates_ready")
        dve_step, act_step, pool_step = sem("dve_step"), sem("act_step"), sem("pool_step")
        pool_waits = sem("pool_waits")
        w_load = [sem(f"w_load{s}") for s in range(2)]
        w_ready = sem("w_ready")
        h_full, h_free = sem("h_full"), sem("h_free")
        hh_ready, hl_ready, pl_ready = sem("hh_ready"), sem("hl_ready"), sem("pl_ready")
        y_full, y_free = sem("y_full"), sem("y_free")
        rows_ready = sem("rows_ready")
        gate_full, gate_free = sem("gate_full"), sem("gate_free")
        weighted_ready, acc_ready = sem("weighted_ready"), sem("acc_ready")

        def hidden_part(part, slot):
            return big[:, slot, part, :, :]

        def q_tile(g):
            return big[:, g % 2, 0, :, :]

        def k_tile(g):
            return big[:, g % 2, 1, :, :]

        def misc(piece):
            n = MISC_USE[piece]
            return misc_bank[n % MISC_BANKS], n

        def wait_full(eng, n):
            eng.wait_ge(misc_full, n + 1)

        def wait_done(eng, piece):
            n = MISC_USE[piece]
            eng.wait_ge(misc_done[n % MISC_BANKS], n // MISC_BANKS + 1)

        def done(n):
            return misc_done[n % MISC_BANKS]

        UPL = BATCHES * UNITS
        HPL = EXPERTS * GROUPS * FC
        YPL = EXPERTS * GROUPS

        def uses_before(layer, kind, g, k=0):
            return (layer * GROUPS + g) * 2 + k

        block = stack.enter_context(nc.Block())

        @block.sync
        def _(sp):
            for layer in range(LAYERS):
                for k in range(4):
                    sp.dma_start(w_raw[:, layer, k, :], wts[layer][k]).then_inc(in_w, 16)
            for layer in range(LAYERS):
                sp.dma_start(rows_raw[layer * B1_ROWS:(layer + 1) * B1_ROWS, :],
                             b1[layer].rearrange("e (c p) -> (e c) p", p=P)).then_inc(in_rows, 16)
                for k in range(2):
                    r = LAYERS * B1_ROWS + 2 * layer + k
                    sp.dma_start(rows_raw[r:r + 1, :], bqk[layer][k].rearrange("(a n) -> a n", a=1)).then_inc(in_rows, 16)
            for g in range(GROUPS):
                bs = slice(g * GROUP, (g + 1) * GROUP)
                sp.dma_start(X[:, bs, :], x[bs].rearrange("b t d -> t b d")).then_inc(in_x[g], 16)
                sp.dma_start(ctx_raw[:, bs, :], ctx_in[bs].rearrange("b t d -> t b d")).then_inc(in_ctx[g], 16)

            def load_expert(layer, e, slot):
                sp.dma_start(w1_raw[:, slot, :], w1[layer][e]).then_inc(w_load[slot], 16)
                sp.dma_start(w2_raw[:, slot, :, :], w2[layer][e].rearrange("(c p) d -> p c d", p=P)).then_inc(w_load[slot], 16)

            for slot in range(2):
                load_expert(0, slot, slot)
            sp.wait_ge(delta_ready, 2)
            for i in range(HG):
                for k, src in enumerate((f32(delta_hi[:, :]), delta_lo[:, :])):
                    r = HROWS * i + ROW_ONE + k
                    sp.dma_start(k_extra[r:r + 1, :], src).then_inc(extra_ready, 16)
            for layer in range(LAYERS):
                first = layer * EXPERTS
                with sp.Fori(0, EXPERTS // 2 - 1) as it:
                    for slot in range(2):
                        sp.wait_ge(w_ready, it * 2 + (first + slot + 1))
                        load_expert(layer, it * 2 + (2 + slot), slot)
                if layer + 1 < LAYERS:
                    for slot in range(2):
                        sp.wait_ge(w_ready, first + EXPERTS - 2 + slot + 1)
                        load_expert(layer + 1, slot, slot)
            for g in range(GROUPS):
                wait_done(sp, ("acc", LAYERS - 1, g))
                bs = slice(g * GROUP, (g + 1) * GROUP)
                sp.dma_start(out[bs].rearrange("b t d -> t b d"), X[:, bs, :]).then_inc(out_done, 16)
            sp.wait_ge(out_done, 16 * GROUPS)

        @block.gpsimd
        def _(pool):
            pool.dma_start(tau_raw[:, :], tau.partition_broadcast(P)).then_inc(in_small, 16)
            pool.dma_start(delta_raw[:, :], delta).then_inc(in_small, 16)
            for layer in range(LAYERS):
                pool.dma_start(bv_all[:, layer, :], bv[layer].partition_broadcast(P)).then_inc(in_small, 16)
                pool.dma_start(bo_all[:, layer, :], bo[layer].partition_broadcast(P)).then_inc(in_small, 16)
                pool.dma_start(wg_raw[:, layer, :], wg[layer]).then_inc(in_small, 16)
                for k in range(2):
                    pool.dma_start(b2_sb[k * EXPERTS:(k + 1) * EXPERTS, layer, :], b2[layer]).then_inc(in_small, 16)
            pool.dma_start(bg_all[:, :], bg.partition_broadcast(P)).then_inc(in_small, 16)
            pool.sem_inc(pl_ready, 1)
            pool.memset(ident[:, :], 0.0).then_inc(pool_step, 1)
            pool.memset(lower[:, :, :], 1.0).then_inc(pool_step, 1)
            pool.wait_ge(pool_step, 2)
            pool.affine_select(out=ident[:, :], in_=ident[:, :], compare_op=ALU.not_equal, fill=1.0,
                               base=0, pattern=[[-1, P]], channel_multiplier=1).then_inc(const_ready, 1)
            pool.affine_select(out=lower[:, :, :], in_=lower[:, :, :], compare_op=ALU.is_gt, fill=0.0, base=0,
                               pattern=[[1, EXPERTS], [-1, EXPERTS]], channel_multiplier=0).then_inc(const_ready, 1)
            for sel in (sel_q_hi, sel_q_lo, sel_k_hi, sel_k_lo):
                pool.memset(f32(sel[:, :, :]), 0.0).then_inc(const_ready, 1)
            pool.memset(k_extra[:, :], 0.0).then_inc(const_ready, 1)
            pool.memset(minus_half[:, :], -0.5).then_inc(const_ready, 1)
            pool.memset(v_sb[:, :, :, :, :], 0.0).then_inc(pool_step, 1)
            pool.wait_ge(pool_step, 3)
            pool.memset(v_sb[:, :, :, :, HD:HD + 1], 1.0).then_inc(const_ready, 1)
            pool.memset(f32(ones[:, :]), 1.0).then_inc(const_ready, 1)
            pool.memset(max_cols[:, :, :], 0.0).then_inc(const_ready, 1)

            def split_expert(layer, e, slot, first_use):
                pool.wait_ge(w_load[slot], first_use)
                pool.sem_inc(pool_waits, 1)
                for raw, hi in ((w1_raw, w1_hi), (w2_raw, w2_hi)):
                    r, h = raw[:, slot], hi[:, slot]
                    pool.tensor_copy(h, r).then_inc(pool_step, 1)

            def split_expert_lo(slot):
                for raw, hi, lo, ready in ((w1_raw, w1_hi, w1_lo, None), (w2_raw, w2_hi, w2_lo, w_ready)):
                    ins = pool.tensor_tensor(lo[:, slot], raw[:, slot], f32(hi[:, slot]), ALU.subtract)
                    if ready is not None:
                        ins.then_inc(ready, 1)

            step = 3
            for slot in range(2):
                split_expert(0, slot, slot, 32)
                step += 2
                pool.wait_ge(pool_step, step)
                split_expert_lo(slot)
            for layer in range(LAYERS):
                for piece in ORDER[layer]:
                    kind, g = piece[0], piece[2]
                    if kind in ("ln1", "ln2"):
                        n = uses_before(layer, kind, g, kind == "ln2")
                        n = LN_INDEX[piece]
                        pool.wait_ge(var_ready, n + 1)
                        pool.tensor_tensor(rstd[:, :], var_eps[:, :], minus_half[:, :], ALU.pow).then_inc(rstd_ready, 1)
                        if kind == "ln1":
                            pool.wait_ge(xn_ready, n + 1)
                            if g == 0 and layer == 0:
                                pool.wait_ge(in_small, 16 * N_SMALL)
                            bs = slice(g * GROUP, (g + 1) * GROUP)
                            pool.tensor_tensor(X[:, bs, :], X[:, bs, :],
                                               bo_all[:, layer, :].unsqueeze(1).broadcast_to([P, GROUP, P]),
                                               ALU.add).then_inc(bo_added, 1)
                    if kind in ("kp", "qp"):
                        k = int(kind == "qp")
                        n = SPLIT_INDEX[piece]
                        if n >= 2:
                            last = ("qs" if k else "ks", *SPLITS[n - 2][1:], HG - 1)
                            wait_full(pool, MISC_USE[last])
                        pool.wait_ge(part_hi_ready, n + 1)
                        pool.tensor_tensor(part_lo[:, k, :], full[:, k, :], f32(part_hi[:, k, :]),
                                           ALU.subtract).then_inc(part_lo_ready, 1)
                pairs, per = EXPERTS // 2, 2 * GROUPS
                if layer:
                    wait_full(pool, MISC_USE[("acc", layer - 1, GROUPS - 1)])
                pool.memset(acc[:, :], 0.0).then_inc(acc_ready, 1)

                def split_odd(it, slot, g):
                    u = slot * GROUPS + g
                    for c in range(1, FC, 2):
                        pool.wait_ge(hh_ready, it * (per * FC) + (layer * HPL + u * FC + c + 1))
                        pool.tensor_tensor(hidden_part(1, u % 2)[:, c, :], hidden[:, c % 2, :],
                                           f32(hidden_part(0, u % 2)[:, c, :]), ALU.subtract).then_inc(pl_ready, 1)

                def accumulate(it, slot, g):
                    u = slot * GROUPS + g
                    ts = slice(g * GT, (g + 1) * GT)
                    pool.wait_ge(y_free, it * per + (layer * YPL + u + 1 + Y_BANKS))
                    pool.wait_ge(acc_ready, it * per + (layer * (YPL + 1) + u + 1))
                    pool.tensor_tensor(acc[:, ts], acc[:, ts], weighted[:, u % 2, :], ALU.add).then_inc(acc_ready, 1)

                def two_ahead(e, slot, loads, steps):
                    pool.wait_ge(y_full, (e + 1) * GROUPS + layer * YPL)
                    split_expert(layer, e, slot, loads)
                    pool.wait_ge(pool_step, steps)
                    split_expert_lo(slot)

                def expert_pair(it, last_pair, loads, steps):
                    units = [(it, slot, g) for slot in range(2) for g in range(GROUPS)]
                    follow = units[1:] + ([] if last_pair else [(it + 1, 0, 0)])
                    for k, unit in enumerate(units):
                        if k < len(follow):
                            split_odd(*follow[k])
                        accumulate(*unit)
                        if k % GROUPS == GROUPS - 1 and not (last_pair and layer + 1 == LAYERS):
                            slot = k // GROUPS
                            two_ahead(it * 2 + slot, slot, loads, steps + 2 * slot)

                split_odd(0, 0, 0)
                with pool.Fori(0, pairs - 1) as it:
                    expert_pair(it, False, (it + 2) * 32 + layer * pairs * 32, it * 4 + (step + 2))
                step += 4 * (pairs - 1)
                expert_pair(pairs - 1, True, (layer + 1) * pairs * 32 + 32, step + 2)
                step += 4


        @block.tensor
        def _(pe):
            def claim(piece):
                b, n = misc(piece)
                if n >= MISC_BANKS:
                    pe.wait_ge(misc_done[n % MISC_BANKS], n // MISC_BANKS)
                return b

            def product(dst, hi, lo, rhi, rlo):
                pe.matmul(dst, hi, rhi, start=True, stop=False)
                pe.matmul(dst, hi, rlo, start=False, stop=False)
                return pe.matmul(dst, lo, rhi, start=False, stop=True)

            def tokens(b):
                return slice(b * P, (b + 1) * P)

            pe.wait_ge(const_ready, N_CONST)
            pe.wait_ge(in_w, 16 * 4 * LAYERS)
            for layer in range(LAYERS):
                dst = claim(("wT", layer))
                for k in range(4):
                    last = pe.transpose(dst[:, k * P:(k + 1) * P], w_raw[:, layer, k, :], ident[:, :])
                last.then_inc(misc_full, 1)
            pe.wait_ge(in_rows, 16 * 3 * LAYERS)
            dst = claim(("rT",))
            pe.transpose(dst[:, 0:N_ROWS], rows_raw[0:N_ROWS, :], ident[0:N_ROWS, 0:N_ROWS]).then_inc(misc_full, 1)

            for layer in range(LAYERS):
                if layer > 0:
                    pe.wait_ge(h_free, layer * HPL + H_BANKS)
                    pe.wait_ge(y_free, layer * YPL + Y_BANKS)
                    pe.wait_ge(gate_free, layer * YPL)
                for piece in ORDER[layer]:
                    kind = piece[0]
                    g = b = piece[2]
                    grp = slice(g * GT, (g + 1) * GT)
                    if kind == "ctxT":
                        pe.wait_ge(in_ctx[g], 16)
                        dst = claim(piece)
                        for t in range(GROUP):
                            last = pe.transpose(dst[:, tokens(t)], ctx_raw[:, g * GROUP + t, :], ident[:, :])
                        last.then_inc(misc_full, 1)
                    elif kind in ("xT1", "xT2"):
                        pe.wait_ge(xn_ready, LN_INDEX[("ln" + kind[2], layer, g)] + 1)
                        dst = claim(piece)
                        for t in range(GROUP):
                            last = pe.transpose(dst[:, tokens(t)], xn[:, t, :], ident[:, :])
                        last.then_inc(misc_full, 1)
                    elif kind == "kp":
                        wait_done(pe, ("wT", layer))
                        wait_done(pe, ("ctxT", 0, g))
                        dst = claim(piece)
                        product(dst[:, :], w_hi[:, layer, 1, :], w_lo[:, layer, 1, :],
                                ctx_hi[:, grp], ctx_lo[:, grp]).then_inc(misc_full, 1)
                    elif kind == "qp":
                        wait_done(pe, ("xT1", layer, g))
                        dst = claim(piece)
                        product(dst[:, :], w_hi[:, layer, 0, :], w_lo[:, layer, 0, :],
                                xt_hi[:, grp], xt_lo[:, grp]).then_inc(misc_full, 1)
                    elif kind == "vp":
                        dst = claim(piece)
                        for t in range(GROUP):
                            at = tokens(g * GROUP + t)
                            last = product(dst[:, tokens(t)], ctx_hi[:, at], ctx_lo[:, at],
                                           w_hi[:, layer, 2, :], w_lo[:, layer, 2, :])
                        last.then_inc(misc_full, 1)
                    elif kind in ("qs", "ks"):
                        j = piece[3]
                        k = int(kind == "qs")
                        if j == 0:
                            pe.wait_ge(part_lo_ready, SPLIT_INDEX[("qp" if k else "kp", layer, g)] + 1)
                            pe.wait_ge(sel_ready, 1)
                        dst = claim(piece)
                        hi, lo = (sel_q_hi, sel_q_lo) if k else (sel_k_hi, sel_k_lo)
                        pe.matmul(dst[:, :], hi[:, j, :], part_hi[:, k, :], start=True, stop=False)
                        pe.matmul(dst[:, :], lo[:, j, :], part_lo[:, k, :], start=False, stop=True).then_inc(misc_full, 1)
                    elif kind == "A":
                        i = piece[3]
                        n = layer * UPL + b * UNITS + i
                        grp_ = b // GROUP
                        if b % GROUP == 0 and i == 0:
                            for j in range(HG):
                                wait_done(pe, ("qs", layer, grp_, j))
                                wait_done(pe, ("ks", layer, grp_, j))
                        if n >= 2:
                            pe.wait_ge(a_free, n - 1)
                        rows = slice(HROWS * i, HROWS * (i + 1))
                        at = tokens(b % GROUP)
                        for j in range(HG):
                            last = pe.matmul(a_bank[n % 2][:, j * P:(j + 1) * P], q_tile(grp_)[rows, j, at],
                                             k_tile(grp_)[rows, j, at], start=True, stop=True)
                        last.then_inc(a_full, 1)
                    elif kind == "mT":
                        pe.wait_ge(max_ready, layer * BATCHES + b + 1)
                        dst = claim(piece)
                        for j in range(HG):
                            last = pe.transpose(dst[:, j * P:(j + 1) * P], max_cols[:, j, :], ident[:, :])
                        last.then_inc(misc_full, 1)
                    elif kind == "B":
                        i = piece[3]
                        n = layer * UPL + b * UNITS + i
                        if i == 0:
                            wait_done(pe, ("mT", layer, b))
                        if n >= 2:
                            pe.wait_ge(b_free, n - 1)
                        rows = slice(HROWS * i, HROWS * (i + 1))
                        at = tokens(b % GROUP)
                        for j in range(HG):
                            last = pe.matmul(b_bank[n % 2][:, j * P:(j + 1) * P], k_tile(b // GROUP)[rows, j, at],
                                             q2[rows, b % 2, j, :], start=True, stop=True)
                        last.then_inc(b_full, 1)
                    elif kind == "PV":
                        i = piece[3]
                        n = layer * UPL + b * UNITS + i
                        pe.wait_ge(b_free, n + 1)
                        if i == 0:
                            if b % GROUP == 0:
                                wait_done(pe, ("vp", layer, b // GROUP))
                            pe.wait_ge(pv_free, layer * BATCHES + b)
                        for j in range(HG):
                            last = pe.matmul(pv_bank[HW * i:HW * i + VW, j * P:(j + 1) * P],
                                             v_sb[:, (b // GROUP) % 2, b % GROUP, HG * j + i, :],
                                             probs[:, b % 2, i, j, :], start=True, stop=True)
                        if i == UNITS - 1:
                            last.then_inc(pv_full, 1)
                    elif kind == "pT":
                        pe.wait_ge(pv_free, layer * BATCHES + b + 1)
                        dst = claim(piece)
                        for j in range(HG):
                            last = pe.transpose(dst[:, j * P:(j + 1) * P], heads_t[:, j * P:(j + 1) * P], ident[:, :])
                        last.then_inc(misc_full, 1)
                    elif kind == "oT":
                        wait_done(pe, ("pT", layer, b))
                        dst = claim(piece)
                        pe.transpose(dst[:, 0:P], attn[:, :], ident[:, :]).then_inc(misc_full, 1)
                    elif kind == "wo":
                        wait_done(pe, ("oT", layer, b))
                        dst = claim(piece)
                        product(dst[:, 0:P], attn_hi[:, b % 2, :], attn_lo[:, b % 2, :],
                                w_hi[:, layer, 3, :], w_lo[:, layer, 3, :]).then_inc(misc_full, 1)
                    elif kind == "lg":
                        wait_done(pe, ("xT2", layer, g))
                        dst = claim(piece)
                        for t in range(GROUP):
                            at = tokens(g * GROUP + t)
                            last = product(dst[:, t * EXPERTS:(t + 1) * EXPERTS], xt_hi[:, at], xt_lo[:, at],
                                           wg_hi[:, layer, :], wg_lo[:, layer, :])
                        last.then_inc(misc_full, 1)
                    elif kind == "gT":
                        pe.wait_ge(gates_ready, layer * GROUPS + g + 1)
                        dst = claim(piece)
                        for t in range(GROUP):
                            last = pe.transpose(dst[0:2 * EXPERTS, tokens(t)],
                                                gates[:, :, :, g * GROUP + t].rearrange("p k e -> p (k e)"), ident[:, :])
                        last.then_inc(misc_full, 1)
                    elif kind == "b2":
                        wait_done(pe, ("gT", layer, g))
                        dst = claim(piece)
                        for t in range(GROUP):
                            last = pe.matmul(dst[:, tokens(t)], f32(gates_t[:, tokens(g * GROUP + t)]), b2_sb[:, layer, :],
                                             start=True, stop=True)
                        last.then_inc(misc_full, 1)

                pe.wait_ge(a_free, (layer + 1) * UPL)
                pe.wait_ge(b_free, (layer + 1) * UPL)
                pe.wait_ge(pv_free, (layer + 1) * BATCHES)

                def hidden_chunk(it, slot, g, c):
                    n = (slot * GROUPS + g) * FC + c
                    if g == 0 and c == 0:
                        pe.wait_ge(w_ready, it * 2 + (layer * EXPERTS + slot + 1))
                    pe.wait_ge(h_free, it * (2 * GROUPS * FC) + (layer * HPL + n + 1))
                    dst = h_bank[c % H_BANKS][:, :]
                    cs, ts = slice(c * P, (c + 1) * P), slice(g * GT, (g + 1) * GT)
                    product(dst, w1_hi[:, slot, cs], w1_lo[:, slot, cs], xt_hi[:, ts], xt_lo[:, ts]).then_inc(h_full, 1)

                def output_part(it, slot, g, c):
                    u = slot * GROUPS + g
                    if c == 0:
                        pe.wait_ge(y_free, it * (2 * GROUPS) + (layer * YPL + u + 1))
                    ready = (hl_ready, pl_ready)[c % 2]
                    pe.wait_ge(ready, it * (GROUPS * FC) + (layer * HPL // 2 + (u * FC + c) // 2 + 2))
                    dst = y_bank[u % 2][:, :]
                    hi, lo = hidden_part(0, u % 2)[:, c, :], hidden_part(1, u % 2)[:, c, :]
                    pe.matmul(dst, w2_hi[:, slot, c, :], hi, start=(c == 0), stop=False)
                    pe.matmul(dst, w2_lo[:, slot, c, :], hi, start=False, stop=False)
                    last = pe.matmul(dst, w2_hi[:, slot, c, :], lo, start=False, stop=(c == FC - 1))
                    if c == FC - 1:
                        last.then_inc(y_full, 1)

                def spread_gates(it, slot, g):
                    u = slot * GROUPS + g
                    pe.wait_ge(rows_ready, it * (2 * GROUPS) + (layer * YPL + u + 1))
                    pe.wait_ge(gate_free, it * (2 * GROUPS) + (layer * YPL + u))
                    pe.matmul(gate_bank[:, :], ones[:, :], gate_rows[:, u % 2, :],
                              start=True, stop=True).then_inc(gate_full, 1)

                def add_up(g):
                    piece = ("acc", layer, g)
                    pe.wait_ge(acc_ready, (layer + 1) * (YPL + 1) - GROUPS + g + 1)
                    dst = claim(piece)
                    for t in range(GROUP):
                        last = pe.transpose(dst[:, tokens(t)], acc[:, tokens(g * GROUP + t)], ident[:, :])
                    last.then_inc(misc_full, 1)

                def expert_pair(it, last_pair):
                    units = [(it, slot, g) for slot in range(2) for g in range(GROUPS)]
                    follow = units[1:] + ([] if last_pair else [(it + 1, 0, 0)])
                    for k, unit in enumerate(units):
                        spread_gates(*unit)
                        for c in range(FC):
                            if k < len(follow):
                                hidden_chunk(*follow[k], c)
                            output_part(*unit, c)
                        if last_pair and k >= GROUPS + 1:
                            add_up(k - GROUPS - 1)
                    if last_pair:
                        add_up(GROUPS - 1)

                for c in range(FC):
                    hidden_chunk(0, 0, 0, c)
                with pe.Fori(0, EXPERTS // 2 - 1) as it:
                    expert_pair(it, False)
                expert_pair(EXPERTS // 2 - 1, True)

        @block.scalar
        def _(act):
            act.sem_inc(h_free, H_BANKS)
            hi_target = {"wT": lambda p: w_hi[:, p[1], :, :].rearrange("p k n -> p (k n)"),
                         "ctxT": lambda p: ctx_hi[:, p[2] * GT:(p[2] + 1) * GT],
                         "xT1": lambda p: xt_hi[:, p[2] * GT:(p[2] + 1) * GT],
                         "xT2": lambda p: xt_hi[:, p[2] * GT:(p[2] + 1) * GT],
                         "oT": lambda p: attn_hi[:, p[2] % 2, :]}

            def hi_part(piece):
                src, n = misc(piece)
                wait_full(act, n)
                dst = hi_target[piece[0]](piece)
                act.activation(dst, src[:, 0:dst.shape[1]], ACT.Copy).then_inc(hi_ready, 1)

            for layer in range(LAYERS):
                hi_part(("wT", layer))
            src, n = misc(("rT",))
            wait_full(act, n)
            act.activation(cols[:, 0:N_ROWS], src[:, 0:N_ROWS], ACT.Copy).then_inc(done(n), 1)
            for layer in range(LAYERS):
                for piece in ORDER[layer]:
                    kind = piece[0]
                    g = b = piece[2]
                    if kind in hi_target:
                        hi_part(piece)
                    elif kind in ("kp", "qp"):
                        k = int(kind == "qp")
                        n = SPLIT_INDEX[piece]
                        if n >= 2:
                            wait_full(act, MISC_USE[("qs" if k else "ks", *SPLITS[n - 2][1:], HG - 1)])
                        act.wait_ge(full_ready, n + 1)
                        act.activation(part_hi[:, k, :], full[:, k, :], ACT.Copy).then_inc(part_hi_ready, 1)
                    elif kind == "qs":
                        src, n = misc(piece)
                        wait_full(act, n)
                        if piece[3] == 0:
                            act.wait_ge(sel_ready, 1)
                        act.activation(q_tile(g)[:, piece[3], :], src[:, :], ACT.Identity,
                                       bias=one_cols[:, 0:1]).then_inc(done(n), 1)
                    elif kind == "B":
                        i = piece[3]
                        n = layer * UPL + b * UNITS + i
                        act.wait_ge(b_full, n + 1)
                        if i == 0 and layer * BATCHES + b >= 2:
                            act.wait_ge(pv_full, layer * BATCHES + b - 1)
                        act.activation(probs[:, b % 2, i, :, :].rearrange("p j l -> p (j l)"), b_bank[n % 2][:, :],
                                       ACT.Exp).then_inc(b_free, 1)
                    elif kind == "PV" and piece[3] == UNITS - 1:
                        act.wait_ge(pv_full, layer * BATCHES + b + 1)
                        if layer * BATCHES + b >= 1:
                            lb = layer * BATCHES + b - 1
                            wait_full(act, MISC_USE[("pT", lb // BATCHES, lb % BATCHES)])
                        act.activation(heads_t[:, :], pv_bank[:, :], ACT.Copy).then_inc(pv_free, 1)
                    elif kind == "lg":
                        act.wait_ge(shifted_ready, layer * GROUPS + g + 1)
                        act.activation(expd[:, :, :], shifted[:, :, :], ACT.Exp).then_inc(exp_ready, 1)
                    elif kind == "gT":
                        src, n = misc(piece)
                        wait_full(act, n)
                        act.activation(gates_t[:, g * GT:(g + 1) * GT], src[0:2 * EXPERTS, :], ACT.Copy).then_inc(done(n), 1)

                func = (ACT.Relu, ACT.Gelu)[layer]

                def expert_pair(it):
                    per = 2 * GROUPS
                    for slot in range(2):
                        for g in range(GROUPS):
                            u = slot * GROUPS + g
                            for c in range(FC):
                                n = u * FC + c
                                act.wait_ge(h_full, it * (per * FC) + (layer * HPL + n + 1))
                                act.wait_ge((hl_ready, pl_ready)[c % 2],
                                            it * (per * FC // 2) + ((layer * HPL + n) // 2 + 1))
                                act.sem_inc(act_step, 1)
                                col = it * (2 * FC) + (layer * B1_ROWS + slot * FC + c)
                                act.activation(hidden[:, c % 2, :], h_bank[c % H_BANKS][:, :], func,
                                               bias=cols[:, bass.ds(col, 1)]).then_inc(h_free, 1)
                            act.wait_ge(gate_full, it * per + (layer * YPL + u + 1))
                            act.wait_ge(y_free, it * per + (layer * YPL + u + 1))
                            act.activation(gate_all[:, u % 2, :], gate_bank[:, :], ACT.Copy).then_inc(gate_free, 1)

                with act.Fori(0, EXPERTS // 2) as it:
                    expert_pair(it)

        @block.vector
        def _(dve):
            steps = [0]

            def chained(ins):
                steps[0] += 1
                ins.then_inc(dve_step, 1)
                dve.wait_ge(dve_step, steps[0])

            dve.sem_inc(hl_ready, 1)
            dve.sem_inc(y_free, Y_BANKS)
            hi_count = [0]
            split_target = {"wT": lambda p: (w_hi[:, p[1], :, :].rearrange("p k n -> p (k n)"), w_lo[:, p[1], :, :].rearrange("p k n -> p (k n)")),
                            "ctxT": lambda p: tuple(a[:, p[2] * GT:(p[2] + 1) * GT] for a in (ctx_hi, ctx_lo)),
                            "xT1": lambda p: tuple(a[:, p[2] * GT:(p[2] + 1) * GT] for a in (xt_hi, xt_lo)),
                            "xT2": lambda p: tuple(a[:, p[2] * GT:(p[2] + 1) * GT] for a in (xt_hi, xt_lo)),
                            "oT": lambda p: tuple(a[:, p[2] % 2, :] for a in (attn_hi, attn_lo))}

            def lo_part(piece):
                src, n = misc(piece)
                hi, lo = split_target[piece[0]](piece)
                hi_count[0] += 1
                dve.wait_ge(hi_ready, hi_count[0])
                dve.tensor_tensor(lo, src[:, 0:hi.shape[1]], f32(hi), ALU.subtract).then_inc(done(n), 1)

            dve.wait_ge(const_ready, N_CONST)
            heads = ident[:, :].rearrange("p (j i e) -> p j i e", j=HG, i=HG)
            for sel, octets in ((sel_q_hi, (0, 1)), (sel_q_lo, (2,)), (sel_k_hi, (0, 2)), (sel_k_lo, (1,))):
                for r in octets:
                    dve.tensor_copy(sel[:, :, :].rearrange("p j (i r e) -> p j i r e", i=HG, e=HD)[:, :, :, r, :],
                                    heads)
            dve.memset(pv_bank[:, :], 0.0)
            by_row = ident[:, :].rearrange("p (i r) -> p r i", r=HROWS)
            for k, row in enumerate((ROW_ONE, ROW_MAX)):
                dve.tensor_reduce(one_cols[:, k:k + 1], by_row[:, row:row + 2, :], AX.XY, ALU.add)
            dve.tensor_reduce(own_rows[:, :], ident[0:2 * EXPERTS, 0:2 * EXPERTS].rearrange("p (k e) -> p e k", k=2),
                              AX.X, ALU.add)
            dve.wait_ge(in_small, 16 * N_SMALL)
            dve.tensor_copy(wg_hi[:, :, :], wg_raw[:, :, :])
            dve.tensor_scalar(tau_sc[:, :], tau_raw[:, :], SOFTMAX_SCALE, None, ALU.mult)
            chained(dve.tensor_scalar(delta_sc[:, :], delta_raw[:, :], SOFTMAX_SCALE, None, ALU.mult))
            dve.tensor_tensor(wg_lo[:, :, :], wg_raw[:, :, :], f32(wg_hi[:, :, :]), ALU.subtract).then_inc(sel_ready, 1)
            chained(dve.tensor_copy(delta_hi[:, :], delta_sc[:, :]))
            dve.tensor_tensor(delta_lo[:, :], delta_sc[:, :], f32(delta_hi[:, :]), ALU.subtract).then_inc(delta_ready, 1)
            dve.tensor_scalar(k_extra[:, :], k_extra[:, :], one_cols[:, 1:2], None, ALU.add).then_inc(delta_ready, 1)
            for layer in range(LAYERS):
                lo_part(("wT", layer))
            wait_done(dve, ("rT",))

            by_head = max_cols[:, :, :].rearrange("p j (i r) -> p i j r", r=HROWS)
            for layer in range(LAYERS):
                for piece in ORDER[layer]:
                    kind = piece[0]
                    g = b = piece[2]
                    bs = slice(g * GROUP, (g + 1) * GROUP)
                    if kind in ("ln1", "ln2"):
                        n = LN_INDEX[piece]
                        if kind == "ln1" and layer == 0:
                            dve.wait_ge(in_x[g], 16)
                        if n:
                            wait_full(dve, MISC_USE[("xT" + LNS[n - 1][0][2], *LNS[n - 1][1:])])
                        for t in range(GROUP):
                            ins = dve.bn_stats(stats[:, t, :], X[:, g * GROUP + t, :])
                        chained(ins)
                        for t in range(GROUP):
                            ins = dve.bn_aggr(mv[:, t, :], stats[:, t, :])
                        chained(ins)
                        dve.tensor_scalar(var_eps[:, :], mv[:, :, 1], LN_EPS, None, ALU.add).then_inc(var_ready, 1)
                        dve.wait_ge(rstd_ready, n + 1)
                        for t in range(GROUP):
                            ins = dve.tensor_scalar(xn[:, t, :], X[:, g * GROUP + t, :], mv[:, t, 0:1],
                                                    rstd[:, t:t + 1], ALU.subtract, ALU.mult)
                        ins.then_inc(xn_ready, 1)
                    elif kind in split_target:
                        lo_part(piece)
                    elif kind in ("kp", "qp"):
                        k = int(kind == "qp")
                        src, n = misc(piece)
                        m = SPLIT_INDEX[piece]
                        if m >= 2:
                            dve.wait_ge(part_lo_ready, m - 1)
                        wait_full(dve, n)
                        bias = LAYERS * B1_ROWS + 2 * layer + (1 - k)
                        if k:
                            ins = dve.scalar_tensor_tensor(
                                out=full[:, 1, :].rearrange("p (b t) -> p b t", t=P),
                                in0=src[:, :].rearrange("p (b t) -> p b t", t=P), scalar=cols[:, bias:bias + 1],
                                in1=tau_sc[:, bs].unsqueeze(2).broadcast_to([P, GROUP, P]), op0=ALU.add, op1=ALU.mult)
                        else:
                            ins = dve.tensor_scalar(full[:, 0, :], src[:, :], cols[:, bias:bias + 1], None, ALU.add)
                        steps[0] += 1
                        ins.then_inc(dve_step, 1)
                        dve.wait_ge(dve_step, steps[0])
                        dve.sem_inc(full_ready, 1)
                        dve.sem_inc(done(n), 1)
                    elif kind == "vp":
                        src, n = misc(piece)
                        wait_full(dve, n)
                        for t in range(GROUP):
                            ins = dve.tensor_tensor(
                                v_sb[:, g % 2, t, :, 0:HD], src[:, t * P:(t + 1) * P].rearrange("p (h e) -> p h e", e=HD),
                                bv_all[:, layer, :].rearrange("p (h e) -> p h e", e=HD), ALU.add)
                        ins.then_inc(done(n), 1)
                    elif kind == "ks":
                        src, n = misc(piece)
                        wait_full(dve, n)
                        if layer == 0 and g == 0:
                            dve.wait_ge(extra_ready, 16 * 2 * HG)
                        dve.tensor_tensor(k_tile(g)[:, piece[3], :], src[:, :], k_extra[:, g * GT:(g + 1) * GT],
                                          ALU.add).then_inc(done(n), 1)
                    elif kind == "A":
                        i = piece[3]
                        n = layer * UPL + b * UNITS + i
                        dve.wait_ge(a_full, n + 1)
                        dve.tensor_reduce(neg_max[:, i * HG:(i + 1) * HG],
                                          a_bank[n % 2][:, :].rearrange("p (j s) -> p j s", s=P),
                                          AX.X, ALU.max, negate=True).then_inc(a_free, 1)
                        if i == UNITS - 1:
                            dve.wait_ge(a_free, n + 1)
                            m = neg_max[:, :].rearrange("p (i j) -> p i j", j=HG)
                            chained(dve.tensor_copy(by_head[:, :, :, ROW_MAX].bitcast(F32R), m))
                            dve.tensor_tensor(by_head[:, :, :, ROW_MAX + 1], m, by_head[:, :, :, ROW_MAX],
                                              ALU.subtract).then_inc(max_ready, 1)
                    elif kind == "mT":
                        src, n = misc(piece)
                        wait_full(dve, n)
                        at = slice((b % GROUP) * P, (b % GROUP + 1) * P)
                        dve.tensor_tensor(q2[:, b % 2, :, :], src[:, :].rearrange("p (j l) -> p j l", l=P),
                                          f32(q_tile(b // GROUP)[:, :, at]), ALU.add).then_inc(done(n), 1)
                    elif kind == "pT":
                        src, n = misc(piece)
                        wait_full(dve, n)
                        pv = src[:, :].rearrange("p (h e) -> p h e", e=HW)
                        chained(dve.reciprocal(rec[:, :], pv[:, :, HD]))
                        dve.tensor_tensor(attn[:, :].rearrange("p (h e) -> p h e", e=HD), pv[:, :, 0:HD],
                                          rec[:, :].unsqueeze(2).broadcast_to([P, HEADS, HD]), ALU.mult)\
                            .then_inc(done(n), 1)
                    elif kind == "wo":
                        src, n = misc(piece)
                        wait_full(dve, n)
                        if b % GROUP == 0:
                            dve.wait_ge(bo_added, layer * GROUPS + b // GROUP + 1)
                        dve.tensor_tensor(X[:, b, :], src[:, 0:P], X[:, b, :], ALU.add).then_inc(done(n), 1)
                        if b % GROUP == GROUP - 1:
                            wait_done(dve, piece)
                    elif kind == "lg":
                        src, n = misc(piece)
                        wait_full(dve, n)
                        logit_src = src[:, 0:GROUP * EXPERTS].rearrange("p (b e) -> p b e", e=EXPERTS)
                        if layer == 1:
                            ins = dve.tensor_tensor(logits[:, :, :], logit_src,
                                                    bg_all[:, :].unsqueeze(1).broadcast_to([P, GROUP, EXPERTS]), ALU.add)
                        else:
                            ins = dve.tensor_copy(logits[:, :, :], logit_src)
                        ins.then_inc(done(n), 1)
                        wait_done(dve, piece)
                        top, total, rtotal, picked, guarded, rpicked = (gsmall[:, k, :] for k in range(6))

                        def over_experts(a):
                            return a.unsqueeze(2).broadcast_to([P, GROUP, EXPERTS])

                        chained(dve.tensor_reduce(top, logits[:, :, :], AX.X, ALU.max))
                        dve.tensor_tensor(shifted[:, :, :], logits[:, :, :], over_experts(top), ALU.subtract)\
                           .then_inc(shifted_ready, 1)
                        other = logits[:, :, :].unsqueeze(2).broadcast_to([P, GROUP, EXPERTS, EXPERTS])
                        own = logits[:, :, :].unsqueeze(3).broadcast_to([P, GROUP, EXPERTS, EXPERTS])
                        dve.tensor_tensor(cmp_gt[:, :, :, :], other, own, ALU.is_gt)
                        chained(dve.tensor_tensor(cmp_eq[:, :, :, :], other, own, ALU.is_equal))
                        low = lower[:, :, :].rearrange("p a c -> p (a c)").unsqueeze(1).broadcast_to([P, GROUP, EXPERTS * EXPERTS])
                        flat = "p b a c -> p b (a c)"
                        chained(dve.tensor_tensor(cmp_eq[:, :, :, :].rearrange(flat), cmp_eq[:, :, :, :].rearrange(flat), low, ALU.mult))
                        chained(dve.tensor_tensor(cmp_gt[:, :, :, :], cmp_gt[:, :, :, :], cmp_eq[:, :, :, :], ALU.add))
                        dve.tensor_reduce(rank[:, :, :], cmp_gt[:, :, :, :], AX.X, ALU.add)
                        dve.wait_ge(exp_ready, layer * GROUPS + g + 1)
                        weight = expd
                        if layer == 1:
                            chained(dve.tensor_reduce(total, expd[:, :, :], AX.X, ALU.add))
                            chained(dve.reciprocal(rtotal, total))
                            chained(dve.tensor_tensor(shifted[:, :, :], expd[:, :, :], over_experts(rtotal), ALU.mult))
                            weight = shifted
                        else:
                            chained(dve.tensor_copy(total, top))
                        chained(dve.scalar_tensor_tensor(out=numer[:, :, :], in0=rank[:, :, :], scalar=1.5,
                                                         in1=weight[:, :, :], op0=ALU.is_lt, op1=ALU.mult))
                        chained(dve.tensor_reduce(picked, numer[:, :, :], AX.X, ALU.add))
                        chained(dve.tensor_scalar(guarded, picked, GATE_EPS, None, ALU.max))
                        chained(dve.reciprocal(rpicked, guarded))
                        chained(dve.tensor_tensor(gates_full[:, :, :], numer[:, :, :], over_experts(rpicked), ALU.mult))
                        g_hi, g_lo = (gates[:, k, :, bs].rearrange("p e b -> p b e") for k in range(2))
                        chained(dve.tensor_copy(g_hi.bitcast(F32R), gates_full[:, :, :]))
                        dve.tensor_tensor(g_lo, gates_full[:, :, :], g_hi, ALU.subtract).then_inc(gates_ready, 1)
                    elif kind == "b2":
                        src, n = misc(piece)
                        wait_full(dve, n)
                        dve.tensor_tensor(X[:, bs, :], src[:, :].rearrange("p (b d) -> p b d", d=P), X[:, bs, :],
                                          ALU.add).then_inc(done(n), 1)
                        wait_done(dve, piece)

                per = 2 * GROUPS

                def mask_rows(it, slot, g):
                    u = slot * GROUPS + g
                    dve.tensor_scalar(gate_rows[:, u % 2, :], f32(gates_t[:, g * GT:(g + 1) * GT]),
                                      own_rows[:, bass.ds(it * 2 + slot, 1)], None, ALU.mult).then_inc(rows_ready, 1)

                def split_hidden(it, slot, g):
                    u = slot * GROUPS + g
                    for c in range(FC):
                        n = layer * HPL + u * FC + c
                        dve.wait_ge(h_free, it * (per * FC) + (n + 1 + H_BANKS))
                        dve.tensor_copy(hidden_part(0, u % 2)[:, c, :], hidden[:, c % 2, :]).then_inc(hh_ready, 1)
                        if c % 2 == 0:
                            dve.wait_ge(hh_ready, it * (per * FC) + (n + 1))
                            dve.tensor_tensor(hidden_part(1, u % 2)[:, c, :], hidden[:, c % 2, :],
                                              f32(hidden_part(0, u % 2)[:, c, :]), ALU.subtract).then_inc(hl_ready, 1)

                def weigh_output(it, slot, g):
                    u = slot * GROUPS + g
                    dve.wait_ge(y_full, it * per + (layer * YPL + u + 1))
                    dve.wait_ge(gate_free, it * per + (layer * YPL + u + 1))
                    dve.wait_ge(acc_ready, it * per + (layer * (YPL + 1) + u + 0))
                    dve.tensor_tensor(weighted[:, u % 2, :], y_bank[u % 2][:, :], gate_all[:, u % 2, :],
                                      ALU.mult).then_inc(y_free, 1)

                def expert_pair(it, last_pair):
                    units = [(it, slot, g) for slot in range(2) for g in range(GROUPS)]
                    follow = units[1:] + ([] if last_pair else [(it + 1, 0, 0)])
                    for k, unit in enumerate(units):
                        if k < len(follow):
                            mask_rows(*follow[k])
                            split_hidden(*follow[k])
                        weigh_output(*unit)
                        if last_pair and k >= GROUPS + 1:
                            add_up(k - GROUPS - 1)
                    if last_pair:
                        add_up(GROUPS - 1)

                def add_up(g):
                    piece = ("acc", layer, g)
                    src, n = misc(piece)
                    bs = slice(g * GROUP, (g + 1) * GROUP)
                    wait_full(dve, n)
                    dve.tensor_tensor(X[:, bs, :], src[:, :].rearrange("p (b d) -> p b d", d=P), X[:, bs, :],
                                      ALU.add).then_inc(done(n), 1)

                for g in range(GROUPS):
                    wait_done(dve, ("gT", layer, g))
                mask_rows(0, 0, 0)
                split_hidden(0, 0, 0)
                with dve.Fori(0, EXPERTS // 2 - 1) as it:
                    expert_pair(it, False)
                expert_pair(EXPERTS // 2 - 1, True)
                for g in range(GROUPS):
                    wait_done(dve, ("acc", layer, g))


LNS = [p for order in ORDER for p in order if p[0] in ("ln1", "ln2")]
LN_INDEX = {p: n for n, p in enumerate(LNS)}
SPLITS = [p for order in ORDER for p in order if p[0] in ("kp", "qp")]
SPLIT_INDEX = {p: n for n, p in enumerate(SPLITS)}
N_SMALL = 2 + 5 * LAYERS + 1
N_CONST = 11


def kernel(**inputs):
    import concourse.bacc as bacc
    from concourse.bass_utils import run_bass_kernel_spmd

    nc = bacc.Bacc("TRN2", target_bir_lowering=False, num_devices=1)
    arrays, aps = {}, {}
    for name, value in inputs.items():
        a = np.ascontiguousarray(value)
        arrays[f"in_{name}"] = a
        aps[name] = nc.dram_tensor(f"in_{name}", a.shape, mybir.dt.from_np(a.dtype), kind="ExternalInput").ap()
    out = nc.dram_tensor("out_x", (BATCHES, P, P), F32, kind="ExternalOutput").ap()

    def both(part, names):
        return [[aps[f"L{layer}_{part}_{n}"] for n in names] for layer in range(LAYERS)]

    def each(name):
        return [aps[f"L{layer}_{name}"] for layer in range(LAYERS)]

    build(nc, aps["x"], aps["ctx_1024"], aps["condB_tau"], aps["fside_BxS2_0"],
          both("xcond", ("Wq", "Wk", "Wv", "Wo")), each("ffn_b1"), both("xcond", ("bq", "bk")),
          each("xcond_bv"), each("xcond_bo"), each("ffn_Wg"), aps["L1_ffn_bg"], each("ffn_W1"), each("ffn_W2"),
          each("ffn_b2"), out)
    r = run_bass_kernel_spmd(nc, [arrays], core_ids=[0])
    return r.results[0]["out_x"]
```

```python
from contextlib import ExitStack

import numpy as np

import concourse.bass as bass
from concourse import mybir

F32 = mybir.dt.float32
F32R = mybir.dt.float32r
ALU = mybir.AluOpType
ACT = mybir.ActivationFunctionType
AX = mybir.AxisListType

P = 128
LAYERS = 2
BATCHES = 16
GROUP = 4
GROUPS = BATCHES // GROUP
GT = GROUP * P
TOKENS = BATCHES * P
HEADS = 16
HD = P // HEADS
HG = 4
HROWS = P // HG
UNITS = HG
EXPERTS = 8
FF = 512
FC = FF // P
LN_EPS = 1e-5
GATE_EPS = 1e-12
SOFTMAX_SCALE = 1.0 / float(np.sqrt(HD))
MISC_BANKS = 3
H_BANKS = 2
VW = 16
HW = 32
Y_BANKS = 2
ROW_ONE, ROW_MAX = 3 * HD, 3 * HD + 2
B1_ROWS = EXPERTS * FC
MISC = ("wT", "rT", "ctxT", "xT1", "qp", "kp", "vp", "qs", "ks", "mT", "pT", "oT", "wo", "xT2", "lg", "gT",
        "acc")


def attention_order(layer):
    def piece(g, *names):
        return [(n, layer, g) if isinstance(n, str) else (n[0], layer, g, n[1]) for n in names]

    if layer == 0:
        yield from piece(0, "ln1a", "ln1b", "ctxT", "wT", "rT")
    else:
        yield from piece(0, "ln1a", "ln1b")
    yield from piece(0, "xT1", "kp", "qp")
    yield from piece(1, "ln1a")
    yield from piece(0, *[(k, j) for k in ("ks", "qs") for j in range(HG)])
    yield from piece(1, "ln1b")
    yield ("vp", layer, 0)
    grouped = [("ln1a", -7, 0), ("ln1b", -7, 2), ("bo", -7, 2), ("xT1", -7, 3), ("kp", -5, 1), ("qp", -5, 3), ("vp", -3, 3)]
    grouped += [((k, j), at, j) for j in range(HG) for k, at in (("ks", -4), ("qs", -3))]
    grouped += [("ctxT", -5, 0)] if layer == 0 else []
    second = [("xT1", -2, 0), ("kp", -2, 3), ("qp", -1, 1), ("vp", 1, 3)]
    second += [(("ks", j), at, i) for j, (at, i) in enumerate(((-1, 2), (-1, 3), (0, 0), (0, 1)))]
    second += [(("qs", j), at, i) for j, (at, i) in enumerate(((0, 2), (0, 3), (1, 0), (1, 1)))]
    second += [("ctxT", -2, 2)] if layer == 0 else []
    singles = [(-2, 2, ("bo", layer, 0)), (-1, 0, ("bo", layer, 1))]
    singles += [(0, 3, ("wT", 1, 0)), (2, 3, ("w0", 0, 0))] if layer == 0 else [(-1, 2, ("acc", layer - 1, GROUPS - 1))]
    done = [("ln2a", 6, 0), ("ln2b", 6, 2), ("xT2", 6, 3), ("lg", 7, 2), ("lg2", 8, 0), ("lg3", 8, 1), ("gT", 8, 3)]
    for s in range(-2, BATCHES + 2):
        between = [[] for _ in range(UNITS)]
        if 2 <= s < BATCHES + 2:
            for i, name in ((0, "pT"), (1, "oT"), (3, "wo")):
                between[i].append((name, layer, s - 2))
        for g in range(GROUPS):
            for name, at, i in (grouped if g > 1 else []) + done:
                if s == g * GROUP + at:
                    between[i] += piece(g, name)
        for name, at, i in second:
            if s == at:
                between[i] += piece(1, name)
        for at, i, single in singles:
            if s == at:
                between[i].append(single)
        for i in range(UNITS):
            if s + 2 < BATCHES:
                yield ("A", layer, s + 2, i)
            if 0 <= s < BATCHES and i:
                yield ("B", layer, s, i - 1)
            if i == 1 and 0 <= s + 1 < BATCHES:
                yield ("mT", layer, s + 1)
            if 1 <= s <= BATCHES:
                yield ("PV", layer, s - 1, i)
            yield from between[i]
        if 0 <= s < BATCHES:
            yield ("B", layer, s, UNITS - 1)


ATTENTION = [list(attention_order(layer)) for layer in range(LAYERS)]


def slots_of(layer):
    last, g = EXPERTS // 2 - 1, GROUPS - 1
    table = [(0, -1, 0, "pT"), (0, -1, 1, "oT"), (0, -1, 2, "wo"), (0, -1, 3, "ln2a"), (0, 0, 1, "ln2b"), (0, 0, 3, "xT2"),
             (0, 1, 0, "lg"), (0, 1, 1, "lg2"), (0, 1, 2, "lg3"), (0, 2, 1, "gT")]
    table = [(*at, (kind, layer, BATCHES - 1 if kind in ("pT", "oT", "wo") else g)) for *at, kind in table]
    table += [(last, GROUPS + 1 + k, 3, ("acc", layer, k)) for k in range(GROUPS - 1)]
    if layer + 1 < LAYERS:
        table += [(last, k, c, (kind, layer + 1, 0)) for k, c, kind in (
            (1, 0, "kp"), (1, 1, "vp"), (6, 0, "ln1a"), (6, 2, "ln1b"), (7, 1, "xT1"), (7, 2, "qp"))]
        table += [(last, 7, j // 2 * 2 + 1, ("ks", layer + 1, 0, j)) for j in range(HG)]
    slots = {}
    for *at, piece in table:
        slots.setdefault(tuple(at), []).append(piece)
    return slots


SLOTS = [slots_of(layer) for layer in range(LAYERS)]
IN_SLOTS = {piece for slots in SLOTS for pieces in slots.values() for piece in pieces}
ORDER = [[piece for piece in order if piece not in IN_SLOTS] for order in ATTENTION]
SEQUENCE = []
for layer_ in range(LAYERS):
    SEQUENCE += ORDER[layer_] + [p for at in sorted(SLOTS[layer_]) for p in SLOTS[layer_][at]]
SEQUENCE += [("acc", LAYERS - 1, GROUPS - 1)]
MISC_USE = {piece: n for n, piece in enumerate(p for p in SEQUENCE if p[0] in MISC)}


def build(nc, gates_dram, x, ctx_in, tau, delta, wts, b1, bqk, bv, bo, wg, bg, w1, w2, b2, out):
    stack = ExitStack()
    with stack:
        def sb(name, shape, dt=F32):
            return stack.enter_context(nc.sbuf_tensor(name, shape, dt))

        def sem(name):
            return stack.enter_context(nc.semaphore(name))

        def f32(ap):
            return ap.bitcast(F32)

        X = sb("X", [P, BATCHES, P])
        ctx_raw = sb("ctx_raw", [P, 2 * GROUP, P])
        ctx_hi, ctx_lo = sb("ctx_hi", [P, TOKENS], F32R), sb("ctx_lo", [P, TOKENS], F32R)
        xt_hi, xt_lo = sb("xt_hi", [P, TOKENS], F32R), sb("xt_lo", [P, TOKENS], F32R)
        w_hi, w_lo = sb("w_hi", [P, LAYERS, 4, P], F32R), sb("w_lo", [P, LAYERS, 4, P], F32R)
        cols = sb("cols", [P, P])
        B2_ROW = LAYERS * (B1_ROWS + 2)
        N_ROWS = B2_ROW + LAYERS * EXPERTS
        ident = sb("ident", [P, P])
        ident_r = sb("ident_r", [P, P], F32R)
        one_cols = sb("one_cols", [P, 2])
        sel_q_hi, sel_q_lo = sb("sel_q_hi", [P, HG, P], F32R), sb("sel_q_lo", [P, HG, P], F32R)
        sel_k_hi, sel_k_lo = sb("sel_k_hi", [P, HG, P], F32R), sb("sel_k_lo", [P, HG, P], F32R)
        tau_sc = sb("tau_sc", [P, BATCHES])
        tau_raw = sb("tau_raw", [P, BATCHES])
        k_extra = sb("k_extra", [P, TOKENS], F32R)
        bv_all, bo_all = sb("bv_all", [P, LAYERS, P]), sb("bo_all", [P, LAYERS, P])
        wg_raw = sb("wg_raw", [P, LAYERS, EXPERTS])
        wg_hi, wg_lo = sb("wg_hi", [P, LAYERS, EXPERTS], F32R), sb("wg_lo", [P, LAYERS, EXPERTS], F32R)
        bg_all = sb("bg_all", [P, EXPERTS])
        lower = sb("lower", [P, EXPERTS, EXPERTS])
        stats, mv = sb("stats", [P, GROUP, 6]), sb("mv", [P, GROUP, 2])
        var_eps, rstd = sb("var_eps", [P, GROUP]), sb("rstd", [P, GROUP])
        minus_half = sb("minus_half", [P, GROUP])
        xn = sb("xn", [P, GROUP, P])
        full = sb("full", [P, 2, GT])
        part_hi, part_lo = sb("part_hi", [P, 2, GT], F32R), sb("part_lo", [P, 2, GT], F32R)
        big = sb("big", [P, 2, 2, HG, GT], F32R)
        k_apart = sb("k_apart", [P, 2, HG, HG, P], F32R)
        q2 = sb("q2", [P, HG, P], F32R)
        probs = sb("probs", [P, 2, UNITS, HG, P])
        w_raw, rows_raw = probs[:, 0:LAYERS, 0, :, :], probs[:, 0, 1, 0, :]
        delta_raw, delta_sc = probs[0:BATCHES, 0, 1, 1, :], probs[0:BATCHES, 0, 1, 2, :]
        delta_hi, delta_lo = probs[0:BATCHES, 1, 1, 0, :], probs[0:BATCHES, 1, 1, 1, :]
        v_sb = sb("v_sb", [P, 2, GROUP, HEADS, VW])
        heads_t = sb("heads_t", [P, HG * P])
        neg_max = sb("neg_max", [P, 2, HEADS])
        max_cols = sb("max_cols", [P, HG, P], F32R)
        rec = sb("rec", [P, HEADS])
        attn = sb("attn", [P, P])
        attn_hi, attn_lo = sb("attn_hi", [P, 2, P], F32R), sb("attn_lo", [P, 2, P], F32R)
        logits, shifted = sb("logits", [P, GROUP, EXPERTS]), sb("shifted", [P, GROUP, EXPERTS])
        expd, numer = sb("expd", [P, GROUP, EXPERTS]), sb("numer", [P, GROUP, EXPERTS])
        gsmall = sb("gsmall", [P, 6, GROUP])
        cmp_ge, cmp_low = (sb(n, [P, GROUP, EXPERTS, EXPERTS]) for n in ("cmp_ge", "cmp_low"))
        before = cmp_ge
        rank = sb("rank", [P, GROUP, EXPERTS])
        gates = sb("gates", [P, GROUP, EXPERTS])
        gates_t = ctx_raw[0:EXPERTS, :, :].rearrange("p b d -> p (b d)")
        hidden = probs[:, 0, 0:2, :, :].rearrange("p s j l -> p s (j l)")
        gate_all = probs[:, 1, 0:2, :, :].rearrange("p s j l -> p s (j l)")
        weighted = sb("weighted", [P, 2, GT])

        def acc(g):
            return probs[:, g // 2, 2 + g % 2, :, :].rearrange("p j l -> p (j l)")

        w1_raw, w2_raw = sb("w1_raw", [P, 2, FF]), sb("w2_raw", [P, 2, FF])
        split_tiles = sb("split_tiles", [P, 2, 4, FF], F32R)
        q_apart_odd = sb("q_apart_odd", [P, HG, HG * P], F32R)
        w1_hi, w1_lo, w2_hi, w2_lo = (split_tiles[:, :, k, :] for k in range(4))
        q_apart = (split_tiles[:, 1, :, :], q_apart_odd[:, :, :])

        bank = [stack.enter_context(nc.psum_tensor(f"bank{n}", [P, 512], F32)) for n in range(8)]
        a_bank, b_bank, pv_bank, misc_bank = bank[0:2], bank[2:4], bank[4], bank[5:8]
        h_bank, y_bank = bank[0:2], bank[2:4]

        in_small = sem("in_small")
        in_w = [sem(f"in_w{layer}") for layer in range(LAYERS)]
        in_x = [sem(f"in_x{g}") for g in range(GROUPS)]
        in_ctx = [sem(f"in_ctx{g}") for g in range(GROUPS)]
        in_delta, in_rows, out_done = sem("in_delta"), sem("in_rows"), sem("out_done")
        ident_ready = sem("ident_ready")
        const_ready = sem("const_ready")
        sel_ready = sem("sel_ready")
        delta_ready, extra_ready = sem("delta_ready"), sem("extra_ready")
        misc_full = sem("misc_full")
        misc_done = [sem(f"misc_done{n}") for n in range(MISC_BANKS)]
        hi_ready = sem("hi_ready")
        var_ready, rstd_ready = sem("var_ready"), sem("rstd_ready")
        xn_ready, bo_added = sem("xn_ready"), sem("bo_added")
        full_ready, part_hi_ready, part_lo_ready = sem("full_ready"), sem("part_hi_ready"), sem("part_lo_ready")
        a_full, a_free, b_full, b_free = sem("a_full"), sem("a_free"), sem("b_full"), sem("b_free")
        k_apart_ready = [sem(f"k_apart_ready{n}") for n in range(2)]
        q_apart_ready = [sem(f"q_apart_ready{n}") for n in range(2)]
        q_zeros_ready = sem("q_zeros_ready")
        max_ready = sem("max_ready")
        pv_full, pv_free = sem("pv_full"), sem("pv_free")
        shifted_ready, exp_ready, gates_ready = sem("shifted_ready"), sem("exp_ready"), sem("gates_ready")
        compared, before_ready = sem("compared"), sem("before_ready")
        dve_step, act_step, pool_step = sem("dve_step"), sem("act_step"), sem("pool_step")
        w_load = [sem(f"w_load{s}") for s in range(2)]
        w_hi_ready = sem("w_hi_ready")
        w1_ready, w2_ready = sem("w1_ready"), sem("w2_ready")
        h_full, h_free = sem("h_full"), sem("h_free")
        hh_ready, hl_ready, pl_ready = sem("hh_ready"), sem("hl_ready"), sem("pl_ready")
        y_full, y_free = sem("y_full"), sem("y_free")
        gates_out = sem("gates_out")
        gate_all_ready = [sem(f"gate_all_ready{n}") for n in range(2)]
        acc_ready = sem("acc_ready")

        def hidden_part(part, slot):
            return big[:, slot, part, :, :]

        def q_tile(g):
            return big[:, g % 2, 0, :, :]

        def k_tile(g):
            return big[:, g % 2, 1, :, :]

        def misc(piece):
            n = MISC_USE[piece]
            return misc_bank[n % MISC_BANKS], n

        def wait_full(eng, n):
            eng.wait_ge(misc_full, n + 1)

        def wait_done(eng, piece):
            n = MISC_USE[piece]
            eng.wait_ge(misc_done[n % MISC_BANKS], n // MISC_BANKS + 1)

        def done(n):
            return misc_done[n % MISC_BANKS]

        UPL = BATCHES * UNITS
        HPL = EXPERTS * GROUPS * FC
        YPL = EXPERTS * GROUPS

        block = stack.enter_context(nc.Block())

        @block.sync
        def _(sp):
            def load_tokens(g):
                bs = slice(g * GROUP, (g + 1) * GROUP)
                sp.dma_start(X[:, bs, :], x[bs].rearrange("b t d -> t b d")).then_inc(in_x[g], 16)
                if g:
                    if g >= 2:
                        wait_full(sp, MISC_USE[("ctxT", 0, g - 2)])
                    sp.dma_start(ctx_raw[:, (g % 2) * GROUP:(g % 2 + 1) * GROUP, :], ctx_in[bs].rearrange("b t d -> t b d")).then_inc(in_ctx[g], 16)

            def load_weights(layer):
                for k in range(4):
                    sp.dma_start(w_raw[:, layer, k, :], wts[layer][k]).then_inc(in_w[layer], 16)

            load_tokens(0)
            load_weights(0)
            for layer in range(LAYERS):
                for k in range(2):
                    r = LAYERS * B1_ROWS + 2 * layer + k
                    sp.dma_start(rows_raw[r:r + 1, :], bqk[layer][k].rearrange("(a n) -> a n", a=1)).then_inc(in_rows, 16)
            load_tokens(1)

            def load_expert(layer, e, slot):
                sp.dma_start(w1_raw[:, slot, :], w1[layer][e]).then_inc(w_load[slot], 16)
                sp.dma_start(w2_raw[:, slot, :].rearrange("p (c d) -> p c d", c=FC),
                             w2[layer][e].rearrange("(c p) d -> p c d", p=P)).then_inc(w_load[slot], 16)

            sp.wait_ge(delta_ready, 1)
            sp.wait_ge(const_ready, ZERO_EXTRA)
            for i in range(HG):
                for k, src in enumerate((delta_hi[:, :], delta_lo[:, :])):
                    r = HROWS * i + ROW_ONE + k
                    sp.dma_start(f32(k_extra[r:r + 1, :]), src).then_inc(extra_ready, 16)
            for layer in range(LAYERS):
                sp.dma_start(bo_all[:, layer, :], bo[layer].partition_broadcast(P)).then_inc(in_small, 16)
                sp.dma_start(bv_all[:, layer, :], bv[layer].partition_broadcast(P)).then_inc(in_small, 16)
                sp.dma_start(wg_raw[:, layer, :], wg[layer]).then_inc(in_small, 16)
            sp.dma_start(bg_all[:, :], bg.partition_broadcast(P)).then_inc(in_small, 16)
            for layer in range(LAYERS):
                def spread_k(b):
                    n = layer * BATCHES + b
                    if n == 0:
                        sp.wait_ge(const_ready, N_CONST)
                    if b % GROUP == 0:
                        for j in range(HG):
                            wait_done(sp, ("ks", layer, b // GROUP, j))
                    if n >= 2:
                        sp.wait_ge(a_full, (n - 1) * UNITS)
                    at = slice((b % GROUP) * P, (b % GROUP + 1) * P)
                    for i in range(HG):
                        rows = slice(HROWS * i, HROWS * (i + 1))
                        sp.dma_start(f32(k_apart[rows, n % 2, :, i, :]), f32(k_tile(b // GROUP)[rows, :, at]))\
                          .then_inc(k_apart_ready[n % 2], 16)

                def spread_q(b):
                    n = layer * BATCHES + b
                    wait_done(sp, ("mT", layer, b))
                    if b == 0:
                        sp.wait_ge(q_zeros_ready, layer + 2)
                    if n >= 2:
                        sp.wait_ge(b_full, (n - 1) * UNITS)
                    for i in range(HG):
                        rows = slice(HROWS * i, HROWS * (i + 1))
                        sp.dma_start(f32(q_apart[n % 2][rows, :, i * P:(i + 1) * P]), f32(q2[rows, :, :]))\
                          .then_inc(q_apart_ready[n % 2], 16)

                def store_gates(g):
                    wait_done(sp, ("gT", layer, g))
                    if layer or g:
                        sp.wait_ge(gates_out, 16 * (layer * GROUPS + g))
                    sp.dma_start(gates_dram[layer][:, g * GT:(g + 1) * GT], gates_t[:, (g % 2) * GT:(g % 2 + 1) * GT]).then_inc(gates_out, 16)

                spread_k(0)
                spread_k(1)
                if layer == 0:
                    load_weights(1)
                    for g in range(2, GROUPS):
                        load_tokens(g)
                    load_expert(0, 0, 0)
                for b in range(BATCHES):
                    if b + 2 < BATCHES:
                        spread_k(b + 2)
                    spread_q(b)
                    if b >= 2 * GROUP + 1 and b % GROUP == 1:
                        store_gates((b - 2 * GROUP - 1) // GROUP)
                sp.wait_ge(b_full, (layer + 1) * UPL)
                load_expert(layer, 1, 1)

                def spread_gates(it, slot, g):
                    u = slot * GROUPS + g
                    sp.wait_ge(y_free, it * (2 * GROUPS) + (layer * YPL + u + 1))
                    sp.dma_start(gate_all[:, u % 2, :],
                                 gates_dram[layer][it * 2 + slot, g * GT:(g + 1) * GT].partition_broadcast(P))\
                      .then_inc(gate_all_ready[u % 2], 16)

                def expert_pair(it):
                    for slot in range(2):
                        for g in range(GROUPS):
                            if isinstance(it, int) and it == 0 and slot == 0:
                                if g == GROUPS - 1:
                                    store_gates(g)
                                sp.wait_ge(gates_out, 16 * (layer * GROUPS + max(g + 1, GROUPS - 1)))
                            if g == 0:
                                last = isinstance(it, int) and it == EXPERTS // 2 - 1
                                if not last or (layer + 1 < LAYERS and slot == 0):
                                    sp.wait_ge(w2_ready, it * 2 + (layer * EXPERTS + slot + 1))
                                    if last:
                                        load_expert(layer + 1, slot, slot)
                                    else:
                                        load_expert(layer, it * 2 + (2 + slot), slot)
                            spread_gates(it, slot, g)

                sp.wait_ge(pv_full, (layer + 1) * BATCHES)
                store_gates(GROUPS - 2)
                expert_pair(0)
                with sp.Fori(1, EXPERTS // 2 - 1) as it:
                    expert_pair(it)
                expert_pair(EXPERTS // 2 - 1)
            for g in range(GROUPS):
                wait_done(sp, ("acc", LAYERS - 1, g))
                bs = slice(g * GROUP, (g + 1) * GROUP)
                sp.dma_start(out[bs].rearrange("b t d -> t b d"), X[:, bs, :]).then_inc(out_done, 16)
            sp.wait_ge(out_done, 16 * GROUPS)

        @block.gpsimd
        def _(pool):
            pool.sem_inc(pl_ready, 1)
            pool.memset(ident[:, :], 0.0).then_inc(pool_step, 1)
            pool.wait_ge(pool_step, 1)
            pool.affine_select(out=ident[:, :], in_=ident[:, :], compare_op=ALU.not_equal, fill=1.0,
                               base=0, pattern=[[-1, P]], channel_multiplier=1).then_inc(ident_ready, 1)
            pool.memset(minus_half[:, :], -0.5)
            for sel in (sel_q_hi, sel_q_lo, sel_k_hi, sel_k_lo):
                pool.memset(f32(sel[:, :, :]), 0.0).then_inc(const_ready, 1)
            pool.memset(f32(k_extra[:, :]), 0.0).then_inc(const_ready, 1)

            def late_constants():
                pool.memset(lower[:, :, :], 1.0).then_inc(pool_step, 1)
                pool.wait_ge(pool_step, 2)
                pool.affine_select(out=lower[:, :, :], in_=lower[:, :, :], compare_op=ALU.is_gt, fill=0.0, base=0,
                                   pattern=[[1, EXPERTS], [-1, EXPERTS]], channel_multiplier=0).then_inc(const_ready, 1)
                pool.memset(f32(max_cols[:, :, :]), 0.0).then_inc(const_ready, 1)
                pool.memset(f32(k_apart[:, :, :, :, :]), 0.0).then_inc(const_ready, 1)
                for tiles in q_apart:
                    pool.memset(f32(tiles), 0.0).then_inc(q_zeros_ready, 1)

            steps = [2]

            def chained(ins):
                steps[0] += 1
                ins.then_inc(pool_step, 1)
                pool.wait_ge(pool_step, steps[0])

            def run(piece):
                layer = piece[1]
                kind, g = piece[0], piece[2]
                if kind in ("ln1a", "ln2a"):
                    if LN_INDEX[piece] == 0:
                        pool.wait_ge(const_ready, ZERO_EXTRA)
                    pool.wait_ge(var_ready, LN_INDEX[piece] + 1)
                    pool.tensor_tensor(rstd[:, :], var_eps[:, :], minus_half[:, :], ALU.pow).then_inc(rstd_ready, 1)
                    if LN_INDEX[piece] == 0:
                        late_constants()
                if kind == "bo" and g == 0 and layer:
                    pool.wait_ge(y_full, layer * YPL)
                    pool.memset(f32(q_apart[0]), 0.0).then_inc(q_zeros_ready, 1)
                if kind == "bo":
                    pool.wait_ge(xn_ready, LN_INDEX[("ln1a", layer, g)] + 1)
                    if g == 0 and layer == 0:
                        pool.wait_ge(in_small, 16 * N_SMALL)
                    bs = slice(g * GROUP, (g + 1) * GROUP)
                    pool.tensor_tensor(X[:, bs, :], X[:, bs, :],
                                       bo_all[:, layer, :].unsqueeze(1).broadcast_to([P, GROUP, P]),
                                       ALU.add).then_inc(bo_added, 1)
                if kind == "lg":
                    pool.wait_ge(compared, layer * GROUPS + g + 1)
                    for t in range(GROUP):
                        ins = pool.tensor_tensor(cmp_low[:, t, :, :], cmp_ge[:, t, :, :], lower[:, :, :], ALU.mult)
                    chained(ins)
                    for t in range(GROUP):
                        ins = pool.tensor_tensor(before[:, t, :, :], lower[:, :, :].rearrange("p a c -> p c a"),
                                                 cmp_low[:, t, :, :].rearrange("p a c -> p c a"), ALU.subtract)
                    chained(ins)
                    pool.tensor_tensor(before[:, :, :, :], before[:, :, :, :], cmp_low[:, :, :, :],
                                       ALU.add).then_inc(before_ready, 1)
                if kind in ("kp", "qp") and g:
                    k = int(kind == "qp")
                    n = SPLIT_INDEX[piece]
                    if n >= 2:
                        last = ("qs" if k else "ks", *SPLITS[n - 2][1:], HG - 1)
                        wait_full(pool, MISC_USE[last])
                    pool.wait_ge(part_hi_ready, n + 1)
                    pool.tensor_tensor(part_lo[:, k, :], full[:, k, :], f32(part_hi[:, k, :]),
                                       ALU.subtract).then_inc(part_lo_ready, 1)

            def slot_pieces(it, k, c):
                if isinstance(it, int):
                    for piece in SLOTS[layer].get((it, k, c), ()):
                        run(piece)

            for layer in range(LAYERS):
                for piece in ORDER[layer]:
                    run(piece)
                pairs, per = EXPERTS // 2, 2 * GROUPS
                if layer:
                    wait_full(pool, MISC_USE[("acc", layer - 1, GROUPS - 1)])

                def split_odd(it, slot, g, c):
                    u = slot * GROUPS + g
                    pool.wait_ge(hh_ready, it * (per * FC) + (layer * HPL + u * FC + c + 1))
                    pool.tensor_tensor(hidden_part(1, u % 2)[:, c, :], hidden[:, c % 2, :],
                                       f32(hidden_part(0, u % 2)[:, c, :]), ALU.subtract).then_inc(pl_ready, 1)

                def accumulate(it, slot, g):
                    u = slot * GROUPS + g
                    pool.wait_ge(y_free, it * per + (layer * YPL + u + 1 + Y_BANKS))
                    pool.wait_ge(acc_ready, it * per + (layer * (YPL + 1) + u + 1))
                    pool.tensor_tensor(acc(g), acc(g), weighted[:, u % 2, :], ALU.add).then_inc(acc_ready, 1)

                def expert_pair(it):
                    units = [(it, slot, g) for slot in range(2) for g in range(GROUPS)]
                    follow = units[1:] + ([] if isinstance(it, int) and it == EXPERTS // 2 - 1 else [(it + 1, 0, 0)])
                    for k, unit in enumerate(units):
                        for c in range(FC):
                            if k < len(follow) and c % 2:
                                split_odd(*follow[k], c)
                            slot_pieces(it, k, c)
                        accumulate(*unit)

                pool.wait_ge(pv_full, (layer + 1) * BATCHES)
                pool.memset(probs[:, :, 2:4, :, :], 0.0).then_inc(acc_ready, 1)
                for c in range(FC):
                    if c % 2:
                        split_odd(0, 0, 0, c)
                    slot_pieces(0, -1, c)
                expert_pair(0)
                with pool.Fori(1, pairs - 1) as it:
                    expert_pair(it)
                expert_pair(pairs - 1)


        @block.tensor
        def _(pe):
            def claim(piece):
                b, n = misc(piece)
                if n >= MISC_BANKS:
                    pe.wait_ge(misc_done[n % MISC_BANKS], n // MISC_BANKS)
                return b

            def product(dst, hi, lo, rhi, rlo):
                pe.matmul(dst, hi, rhi, start=True, stop=False)
                pe.matmul(dst, hi, rlo, start=False, stop=False)
                return pe.matmul(dst, lo, rhi, start=False, stop=True)

            def tokens(b):
                return slice(b * P, (b + 1) * P)

            pe.wait_ge(ident_ready, 1)
            def run(piece):
                layer = piece[1]
                kind = piece[0]
                g = b = piece[2]
                grp = slice(g * GT, (g + 1) * GT)
                if kind == "wT":
                    pe.wait_ge(in_w[layer], 16 * 4)
                    dst = claim(piece)
                    for k in range(4):
                        last = pe.transpose(dst[:, k * P:(k + 1) * P], w_raw[:, layer, k, :], ident[:, :])
                    last.then_inc(misc_full, 1)
                elif kind == "rT":
                    pe.wait_ge(in_rows, 16 * 4 * LAYERS)
                    dst = claim(piece)
                    pe.transpose(dst[:, 0:N_ROWS], rows_raw[0:N_ROWS, :], ident[0:N_ROWS, 0:N_ROWS]).then_inc(misc_full, 1)
                elif kind == "ctxT":
                    pe.wait_ge(in_ctx[g], 16)
                    dst = claim(piece)
                    for t in range(GROUP):
                        last = pe.transpose(dst[:, tokens(t)], ctx_raw[:, (g % 2) * GROUP + t, :], ident[:, :])
                    last.then_inc(misc_full, 1)
                elif kind in ("xT1", "xT2"):
                    pe.wait_ge(xn_ready, LN_INDEX[("ln" + kind[2] + "a", layer, g)] + 1)
                    dst = claim(piece)
                    for t in range(GROUP):
                        last = pe.transpose(dst[:, tokens(t)], xn[:, t, :], ident[:, :])
                    last.then_inc(misc_full, 1)
                elif kind == "kp":
                    wait_done(pe, ("wT", layer, 0))
                    wait_done(pe, ("ctxT", 0, g))
                    dst = claim(piece)
                    product(dst[:, :], w_hi[:, layer, 1, :], w_lo[:, layer, 1, :],
                            ctx_hi[:, grp], ctx_lo[:, grp]).then_inc(misc_full, 1)
                elif kind == "qp":
                    wait_done(pe, ("xT1", layer, g))
                    dst = claim(piece)
                    product(dst[:, :], w_hi[:, layer, 0, :], w_lo[:, layer, 0, :],
                            xt_hi[:, grp], xt_lo[:, grp]).then_inc(misc_full, 1)
                elif kind == "vp":
                    dst = claim(piece)
                    for t in range(GROUP):
                        at = tokens(g * GROUP + t)
                        last = product(dst[:, tokens(t)], ctx_hi[:, at], ctx_lo[:, at],
                                       w_hi[:, layer, 2, :], w_lo[:, layer, 2, :])
                    last.then_inc(misc_full, 1)
                elif kind in ("qs", "ks"):
                    j = piece[3]
                    k = int(kind == "qs")
                    if j == 0:
                        pe.wait_ge(part_lo_ready, SPLIT_INDEX[("qp" if k else "kp", layer, g)] + 1)
                        pe.wait_ge(sel_ready, 1)
                    dst = claim(piece)
                    hi, lo = (sel_q_hi, sel_q_lo) if k else (sel_k_hi, sel_k_lo)
                    pe.matmul(dst[:, :], hi[:, j, :], part_hi[:, k, :], start=True, stop=False)
                    last = pe.matmul(dst[:, :], lo[:, j, :], part_lo[:, k, :], start=False, stop=bool(k))
                    if not k:
                        if layer == 0 and g == 0 and j == 0:
                            pe.wait_ge(extra_ready, 16 * 2 * HG)
                        last = pe.matmul(dst[:, :], ident_r[:, :], k_extra[:, grp], start=False, stop=True)
                    last.then_inc(misc_full, 1)
                elif kind == "A":
                    i = piece[3]
                    n = layer * UPL + b * UNITS + i
                    grp_ = b // GROUP
                    if b % GROUP == 0 and i == 0:
                        for j in range(HG):
                            wait_done(pe, ("qs", layer, grp_, j))
                    if n >= 2:
                        pe.wait_ge(a_free, n - 1)
                    m = layer * BATCHES + b
                    if i == 0:
                        pe.wait_ge(k_apart_ready[m % 2], (m // 2 + 1) * 16 * HG)
                    pe.matmul(a_bank[n % 2][:, :], q_tile(grp_)[:, i, tokens(b % GROUP)],
                              k_apart[:, m % 2, i, :, :].rearrange("p i s -> p (i s)"),
                              start=True, stop=True).then_inc(a_full, 1)
                elif kind == "mT":
                    dst = claim(piece)
                    pe.matmul(dst[:, :].rearrange("p (j l) -> p j l", l=P), ident_r[:, :],
                              q_tile(b // GROUP)[:, :, tokens(b % GROUP)], start=True, stop=False)
                    pe.wait_ge(max_ready, layer * BATCHES + b + 1)
                    for j in range(HG):
                        last = pe.matmul(dst[:, j * P:(j + 1) * P], max_cols[:, j, :], ident_r[:, :],
                                         start=False, stop=(j == HG - 1))
                    last.then_inc(misc_full, 1)
                elif kind == "B":
                    i = piece[3]
                    n = layer * UPL + b * UNITS + i
                    if i == 0:
                        m = layer * BATCHES + b
                        pe.wait_ge(q_apart_ready[m % 2], 16 * HG * (m // 2 + 1))
                    if n >= 2:
                        pe.wait_ge(b_free, n - 1)
                    pe.matmul(b_bank[n % 2][:, :], k_tile(b // GROUP)[:, i, tokens(b % GROUP)],
                              q_apart[(layer * BATCHES + b) % 2][:, i, :], start=True, stop=True).then_inc(b_full, 1)
                elif kind == "PV":
                    i = piece[3]
                    n = layer * UPL + b * UNITS + i
                    pe.wait_ge(b_free, n + 1)
                    if i == 0:
                        if b == 0 and layer == 0:
                            pe.wait_ge(sel_ready, 2)
                        if b % GROUP == 0:
                            wait_done(pe, ("vp", layer, b // GROUP))
                        pe.wait_ge(pv_free, layer * BATCHES + b)
                    for k in range(HG):
                        last = pe.matmul(pv_bank[HW * k:HW * k + VW, i * P:(i + 1) * P],
                                         v_sb[:, (b // GROUP) % 2, b % GROUP, HG * i + k, :],
                                         probs[:, b % 2, i, k, :], start=True, stop=True)
                    if i == UNITS - 1:
                        last.then_inc(pv_full, 1)
                elif kind == "pT":
                    pe.wait_ge(pv_free, layer * BATCHES + b + 1)
                    dst = claim(piece)
                    for j in range(HG):
                        last = pe.transpose(dst[:, j * P:(j + 1) * P], heads_t[:, j * P:(j + 1) * P], ident[:, :])
                    last.then_inc(misc_full, 1)
                elif kind == "oT":
                    wait_done(pe, ("pT", layer, b))
                    dst = claim(piece)
                    pe.transpose(dst[:, 0:P], attn[:, :], ident[:, :]).then_inc(misc_full, 1)
                elif kind == "wo":
                    wait_done(pe, ("oT", layer, b))
                    dst = claim(piece)
                    product(dst[:, 0:P], attn_hi[:, b % 2, :], attn_lo[:, b % 2, :],
                            w_hi[:, layer, 3, :], w_lo[:, layer, 3, :]).then_inc(misc_full, 1)
                elif kind == "lg":
                    wait_done(pe, ("xT2", layer, g))
                    dst = claim(piece)
                    for t in range(GROUP):
                        at = tokens(g * GROUP + t)
                        last = product(dst[:, t * EXPERTS:(t + 1) * EXPERTS], xt_hi[:, at], xt_lo[:, at],
                                       wg_hi[:, layer, :], wg_lo[:, layer, :])
                    last.then_inc(misc_full, 1)
                elif kind == "gT":
                    pe.wait_ge(gates_ready, layer * GROUPS + g + 1)
                    dst = claim(piece)
                    for t in range(GROUP):
                        last = pe.transpose(dst[0:EXPERTS, tokens(t)], gates[:, t, :], ident[:, :])
                    last.then_inc(misc_full, 1)
                elif kind == "acc":
                    pe.wait_ge(acc_ready, (layer + 1) * (YPL + 1) - GROUPS + g + 1)
                    dst = claim(piece)
                    for t in range(GROUP):
                        last = pe.transpose(dst[:, tokens(t)], acc(g)[:, tokens(t)], ident[:, :])
                    last.then_inc(misc_full, 1)

            def slot_pieces(it, k, c):
                if isinstance(it, int):
                    for piece in SLOTS[layer].get((it, k, c), ()):
                        run(piece)

            for layer in range(LAYERS):
                if layer > 0:
                    pe.wait_ge(h_free, layer * HPL + H_BANKS)
                    pe.wait_ge(y_free, layer * YPL + Y_BANKS)
                for piece in ORDER[layer]:
                    run(piece)
                pe.wait_ge(a_free, (layer + 1) * UPL)
                pe.wait_ge(b_free, (layer + 1) * UPL)

                def hidden_chunk(it, slot, g, c):
                    n = (slot * GROUPS + g) * FC + c
                    if g == 0 and c == 0:
                        pe.wait_ge(w1_ready, it * 2 + (layer * EXPERTS + slot + 1))
                    pe.wait_ge(h_free, it * (2 * GROUPS * FC) + (layer * HPL + n + 1))
                    dst = h_bank[c % H_BANKS][:, :]
                    cs, ts = slice(c * P, (c + 1) * P), slice(g * GT, (g + 1) * GT)
                    product(dst, w1_hi[:, slot, cs], w1_lo[:, slot, cs], xt_hi[:, ts], xt_lo[:, ts]).then_inc(h_full, 1)

                def output_part(it, slot, g, c):
                    u = slot * GROUPS + g
                    if g == 0 and c == 0:
                        pe.wait_ge(w2_ready, it * 2 + (layer * EXPERTS + slot + 1))
                    if c == 0:
                        pe.wait_ge(y_free, it * (2 * GROUPS) + (layer * YPL + u + 1))
                    ready = (hl_ready, pl_ready)[c % 2]
                    pe.wait_ge(ready, it * (GROUPS * FC) + (layer * HPL // 2 + (u * FC + c) // 2 + 2))
                    dst = y_bank[u % 2][:, :]
                    hi, lo = hidden_part(0, u % 2)[:, c, :], hidden_part(1, u % 2)[:, c, :]
                    pe.matmul(dst, w2_hi[:, slot, c * P:(c + 1) * P], hi, start=(c == 0), stop=False)
                    pe.matmul(dst, w2_lo[:, slot, c * P:(c + 1) * P], hi, start=False, stop=False)
                    last = pe.matmul(dst, w2_hi[:, slot, c * P:(c + 1) * P], lo, start=False, stop=(c == FC - 1))
                    if c == FC - 1:
                        last.then_inc(y_full, 1)

                def expert_pair(it):
                    units = [(it, slot, g) for slot in range(2) for g in range(GROUPS)]
                    follow = units[1:] + ([] if isinstance(it, int) and it == EXPERTS // 2 - 1 else [(it + 1, 0, 0)])
                    for k, unit in enumerate(units):
                        for c in range(FC):
                            if k < len(follow):
                                hidden_chunk(*follow[k], c)
                            output_part(*unit, c)
                            slot_pieces(it, k, c)

                for c in range(FC):
                    hidden_chunk(0, 0, 0, c)
                    slot_pieces(0, -1, c)
                expert_pair(0)
                with pe.Fori(1, EXPERTS // 2 - 1) as it:
                    expert_pair(it)
                expert_pair(EXPERTS // 2 - 1)
                if layer + 1 == LAYERS:
                    run(("acc", layer, GROUPS - 1))

        @block.scalar
        def _(act):
            act.sem_inc(h_free, H_BANKS)
            act.dma_start(ctx_raw[:, 0:GROUP, :], ctx_in[0:GROUP].rearrange("b t d -> t b d")).then_inc(in_ctx[0], 16)
            act.dma_start(delta_raw[:, :], delta).then_inc(in_delta, 16)
            act.dma_start(tau_raw[:, :], tau.partition_broadcast(P)).then_inc(in_delta, 16)
            for layer in range(LAYERS):
                act.dma_start(rows_raw[layer * B1_ROWS:(layer + 1) * B1_ROWS, :],
                              b1[layer].rearrange("e (c p) -> (e c) p", p=P)).then_inc(in_rows, 16)
                r = B2_ROW + layer * EXPERTS
                act.dma_start(rows_raw[r:r + EXPERTS, :], b2[layer]).then_inc(in_rows, 16)
            hi_target = {"wT": lambda p: w_hi[:, p[1], :, :].rearrange("p k n -> p (k n)"),
                         "ctxT": lambda p: ctx_hi[:, p[2] * GT:(p[2] + 1) * GT],
                         "xT1": lambda p: xt_hi[:, p[2] * GT:(p[2] + 1) * GT],
                         "xT2": lambda p: xt_hi[:, p[2] * GT:(p[2] + 1) * GT],
                         "oT": lambda p: attn_hi[:, p[2] % 2, :]}

            def hi_part(piece):
                src, n = misc(piece)
                wait_full(act, n)
                dst = hi_target[piece[0]](piece)
                act.activation(dst, src[:, 0:dst.shape[1]], ACT.Copy).then_inc(hi_ready, 1)

            def split_weights(k, slot):
                raw, hi = ((w1_raw, w1_hi), (w2_raw, w2_hi))[k]
                src, dst = raw[:, slot], hi[:, slot]
                act.activation(dst, src, ACT.Copy).then_inc(w_hi_ready, 1)

            def run(piece):
                layer = piece[1]
                kind = piece[0]
                g = b = piece[2]
                if kind in hi_target:
                    hi_part(piece)
                elif kind == "rT":
                    src, n = misc(piece)
                    wait_full(act, n)
                    act.activation(cols[:, 0:N_ROWS], src[:, 0:N_ROWS], ACT.Copy).then_inc(done(n), 1)
                elif kind == "w0":
                    act.wait_ge(w_load[0], 32)
                    for k in range(2):
                        split_weights(k, 0)
                elif kind in ("kp", "qp"):
                    k = int(kind == "qp")
                    n = SPLIT_INDEX[piece]
                    if n >= 2:
                        wait_full(act, MISC_USE[("qs" if k else "ks", *SPLITS[n - 2][1:], HG - 1)])
                    act.wait_ge(full_ready, n + 1)
                    act.activation(part_hi[:, k, :], full[:, k, :], ACT.Copy).then_inc(part_hi_ready, 1)
                elif kind == "ks":
                    src, n = misc(piece)
                    wait_full(act, n)
                    if g == 0 and piece[3] == 0:
                        act.wait_ge(sel_ready, 1)
                    act.activation(k_tile(g)[:, piece[3], :], src[:, :], ACT.Identity,
                                   bias=one_cols[:, 1:2]).then_inc(done(n), 1)
                elif kind == "mT":
                    src, n = misc(piece)
                    wait_full(act, n)
                    n_batch = layer * BATCHES + b
                    if n_batch:
                        act.wait_ge(q_apart_ready[(n_batch - 1) % 2], 16 * HG * ((n_batch - 1) // 2 + 1))
                    act.activation(q2[:, :, :].rearrange("p j l -> p (j l)"), src[:, :],
                                   ACT.Copy).then_inc(done(n), 1)
                elif kind == "qs":
                    src, n = misc(piece)
                    wait_full(act, n)
                    if piece[3] == 0:
                        act.wait_ge(sel_ready, 1)
                    act.activation(q_tile(g)[:, piece[3], :], src[:, :], ACT.Identity,
                                   bias=one_cols[:, 0:1]).then_inc(done(n), 1)
                elif kind == "B":
                    i = piece[3]
                    n = layer * UPL + b * UNITS + i
                    act.wait_ge(b_full, n + 1)
                    if i == 0 and layer * BATCHES + b >= 2:
                        act.wait_ge(pv_full, layer * BATCHES + b - 1)
                    act.activation(probs[:, b % 2, i, :, :].rearrange("p j l -> p (j l)"), b_bank[n % 2][:, :],
                                   ACT.Exp).then_inc(b_free, 1)
                elif kind == "PV" and piece[3] == UNITS - 1:
                    act.wait_ge(pv_full, layer * BATCHES + b + 1)
                    if layer * BATCHES + b >= 1:
                        lb = layer * BATCHES + b - 1
                        wait_full(act, MISC_USE[("pT", lb // BATCHES, lb % BATCHES)])
                    act.activation(heads_t[:, :], pv_bank[:, :], ACT.Copy).then_inc(pv_free, 1)
                elif kind == "lg":
                    act.wait_ge(shifted_ready, layer * GROUPS + g + 1)
                    act.activation(expd[:, :, :], shifted[:, :, :], ACT.Exp).then_inc(exp_ready, 1)
                elif kind == "gT":
                    src, n = misc(piece)
                    wait_full(act, n)
                    if layer * GROUPS + g >= 2:
                        act.wait_ge(gates_out, 16 * (layer * GROUPS + g - 1))
                    act.activation(gates_t[:, (g % 2) * GT:(g % 2 + 1) * GT], src[0:EXPERTS, :], ACT.Copy).then_inc(done(n), 1)

            def slot_pieces(it, k, c):
                if isinstance(it, int):
                    for piece in SLOTS[layer].get((it, k, c), ()):
                        run(piece)

            for layer in range(LAYERS):
                for piece in ORDER[layer]:
                    run(piece)
                func = (ACT.Relu, ACT.Gelu)[layer]

                def expert_pair(it):
                    per = 2 * GROUPS
                    last_pair = isinstance(it, int) and it == EXPERTS // 2 - 1
                    for slot in range(2):
                        for g in range(GROUPS):
                            u = slot * GROUPS + g
                            if g >= 2 and not (slot and last_pair and layer + 1 == LAYERS):
                                loads = (layer * EXPERTS // 2 + slot + 1) * 32
                                act.wait_ge(w_load[1 - slot], it * 32 + loads)
                                act.wait_ge(y_full, it * per + (layer * YPL + slot * GROUPS + 1))
                                split_weights(g - 2, 1 - slot)
                            for c in range(FC):
                                n = u * FC + c
                                act.wait_ge(h_full, it * (per * FC) + (layer * HPL + n + 1))
                                act.wait_ge((hl_ready, pl_ready)[c % 2],
                                            it * (per * FC // 2) + ((layer * HPL + n) // 2 + 1))
                                act.sem_inc(act_step, 1)
                                col = it * (2 * FC) + (layer * B1_ROWS + slot * FC + c)
                                act.activation(hidden[:, c % 2, :], h_bank[c % H_BANKS][:, :], func,
                                               bias=cols[:, bass.ds(col, 1)]).then_inc(h_free, 1)
                                slot_pieces(it, u - 1, c)
                    if last_pair:
                        for c in range(FC):
                            slot_pieces(it, per - 1, c)

                expert_pair(0)
                with act.Fori(1, EXPERTS // 2 - 1) as it:
                    expert_pair(it)
                expert_pair(EXPERTS // 2 - 1)

        @block.vector
        def _(dve):
            steps = [0]

            def chained(ins):
                steps[0] += 1
                ins.then_inc(dve_step, 1)
                dve.wait_ge(dve_step, steps[0])

            dve.sem_inc(hl_ready, 1)
            dve.sem_inc(y_free, Y_BANKS)
            hi_count = [0]
            split_target = {"wT": lambda p: (w_hi[:, p[1], :, :].rearrange("p k n -> p (k n)"), w_lo[:, p[1], :, :].rearrange("p k n -> p (k n)")),
                            "ctxT": lambda p: tuple(a[:, p[2] * GT:(p[2] + 1) * GT] for a in (ctx_hi, ctx_lo)),
                            "xT1": lambda p: tuple(a[:, p[2] * GT:(p[2] + 1) * GT] for a in (xt_hi, xt_lo)),
                            "xT2": lambda p: tuple(a[:, p[2] * GT:(p[2] + 1) * GT] for a in (xt_hi, xt_lo)),
                            "oT": lambda p: tuple(a[:, p[2] % 2, :] for a in (attn_hi, attn_lo))}

            def lo_part(piece):
                src, n = misc(piece)
                hi, lo = split_target[piece[0]](piece)
                hi_count[0] += 1
                dve.wait_ge(hi_ready, hi_count[0])
                dve.tensor_tensor(lo, src[:, 0:hi.shape[1]], f32(hi), ALU.subtract).then_inc(done(n), 1)

            def scores_constants():
                dve.wait_ge(ident_ready, 1)
                dve.tensor_copy(ident_r[:, :], ident[:, :])
                by_row = ident[:, :].rearrange("p (i r) -> p r i", r=HROWS)
                for k, row in enumerate((ROW_ONE, ROW_MAX)):
                    dve.tensor_reduce(one_cols[:, k:k + 1], by_row[:, row:row + 2, :], AX.XY, ALU.add)
                dve.wait_ge(const_ready, ZERO_SEL)
                heads = ident[:, :].rearrange("p (j i e) -> p j i e", j=HG, i=HG)
                for sel, octets in ((sel_q_hi, (0, 1)), (sel_q_lo, (2,)), (sel_k_hi, (0, 2)), (sel_k_lo, (1,))):
                    for r in octets:
                        ins = dve.tensor_copy(sel[:, :, :].rearrange("p j (i r e) -> p j i r e", i=HG, e=HD)[:, :, :, r, :],
                                              heads)
                ins.then_inc(sel_ready, 1)
                dve.wait_ge(in_delta, 16 * 2)
                dve.tensor_scalar(tau_sc[:, :], tau_raw[:, :], SOFTMAX_SCALE, None, ALU.mult)
                chained(dve.tensor_scalar(delta_sc[:, :], delta_raw[:, :], SOFTMAX_SCALE, None, ALU.mult))
                chained(dve.tensor_copy(delta_hi.bitcast(F32R), delta_sc[:, :]))
                dve.tensor_tensor(delta_lo[:, :], delta_sc[:, :], delta_hi[:, :], ALU.subtract).then_inc(delta_ready, 1)

            def other_constants():
                dve.memset(v_sb[:, :, :, :, :], 0.0).then_inc(dve_step, 1)
                steps[0] += 1
                dve.wait_ge(in_small, 16 * N_SMALL)
                chained(dve.tensor_copy(wg_hi[:, :, :], wg_raw[:, :, :]))
                dve.tensor_tensor(wg_lo[:, :, :], wg_raw[:, :, :], f32(wg_hi[:, :, :]), ALU.subtract)
                dve.memset(v_sb[:, :, :, :, HD:HD + 1], 1.0)
                dve.memset(pv_bank[:, :], 0.0).then_inc(sel_ready, 1)
                dve.wait_ge(const_ready, N_CONST)

            def split_weights(k, slot):
                raw, hi, lo, ready = ((w1_raw, w1_hi, w1_lo, w1_ready), (w2_raw, w2_hi, w2_lo, w2_ready))[k]
                dve.tensor_tensor(lo[:, slot], raw[:, slot], f32(hi[:, slot]), ALU.subtract).then_inc(ready, 1)

            top, total, rtotal, picked, guarded, rpicked = (gsmall[:, k, :] for k in range(6))

            def over_experts(a):
                return a.unsqueeze(2).broadcast_to([P, GROUP, EXPERTS])

            by_head = max_cols[:, :, :].rearrange("p j (i r) -> p i j r", r=HROWS)

            def run(piece):
                layer = piece[1]
                kind = piece[0]
                g = b = piece[2]
                bs = slice(g * GROUP, (g + 1) * GROUP)
                if kind in ("ln1a", "ln2a"):
                    if kind == "ln1a":
                        if layer:
                            wait_done(dve, ("acc", layer - 1, g))
                        else:
                            dve.wait_ge(in_x[g], 16)
                    for t in range(GROUP):
                        ins = dve.bn_stats(stats[:, t, :], X[:, g * GROUP + t, :])
                    chained(ins)
                    for t in range(GROUP):
                        ins = dve.bn_aggr(mv[:, t, :], stats[:, t, :])
                    chained(ins)
                    dve.tensor_scalar(var_eps[:, :], mv[:, :, 1], LN_EPS, None, ALU.add).then_inc(var_ready, 1)
                elif kind in ("ln1b", "ln2b"):
                    n = LN_INDEX[(kind[:3] + "a", layer, g)]
                    if n:
                        wait_full(dve, MISC_USE[("xT" + LNS[n - 1][0][2], *LNS[n - 1][1:])])
                    dve.wait_ge(rstd_ready, n + 1)
                    for t in range(GROUP):
                        ins = dve.tensor_scalar(xn[:, t, :], X[:, g * GROUP + t, :], mv[:, t, 0:1],
                                                rstd[:, t:t + 1], ALU.subtract, ALU.mult)
                    ins.then_inc(xn_ready, 1)
                    if n == 0:
                        scores_constants()
                elif kind in split_target:
                    lo_part(piece)
                elif kind == "w0":
                    for k in range(2):
                        dve.wait_ge(w_hi_ready, k + 1)
                        split_weights(k, 0)
                elif kind in ("kp", "qp"):
                    k = int(kind == "qp")
                    src, n = misc(piece)
                    m = SPLIT_INDEX[piece]
                    if m >= 2:
                        dve.wait_ge(part_lo_ready, m - 1)
                    wait_full(dve, n)
                    bias = LAYERS * B1_ROWS + 2 * layer + (1 - k)
                    if k:
                        ins = dve.scalar_tensor_tensor(
                            out=full[:, 1, :].rearrange("p (b t) -> p b t", t=P),
                            in0=src[:, :].rearrange("p (b t) -> p b t", t=P), scalar=cols[:, bias:bias + 1],
                            in1=tau_sc[:, bs].unsqueeze(2).broadcast_to([P, GROUP, P]), op0=ALU.add, op1=ALU.mult)
                    else:
                        ins = dve.tensor_scalar(full[:, 0, :], src[:, :], cols[:, bias:bias + 1], None, ALU.add)
                    steps[0] += 1
                    ins.then_inc(dve_step, 1)
                    dve.wait_ge(dve_step, steps[0])
                    dve.sem_inc(full_ready, 1)
                    dve.sem_inc(done(n), 1)
                    if g == 0:
                        if m >= 2:
                            last = ("qs" if k else "ks", *SPLITS[m - 2][1:], HG - 1)
                            wait_full(dve, MISC_USE[last])
                        dve.wait_ge(part_hi_ready, m + 1)
                        dve.tensor_tensor(part_lo[:, k, :], full[:, k, :], f32(part_hi[:, k, :]),
                                          ALU.subtract).then_inc(part_lo_ready, 1)
                elif kind == "vp":
                    if layer == 0 and g == 0:
                        other_constants()
                    src, n = misc(piece)
                    wait_full(dve, n)
                    for t in range(GROUP):
                        ins = dve.tensor_tensor(
                            v_sb[:, g % 2, t, :, 0:HD], src[:, t * P:(t + 1) * P].rearrange("p (h e) -> p h e", e=HD),
                            bv_all[:, layer, :].rearrange("p (h e) -> p h e", e=HD), ALU.add)
                    ins.then_inc(done(n), 1)
                elif kind == "A":
                    i = piece[3]
                    n = layer * UPL + b * UNITS + i
                    dve.wait_ge(a_full, n + 1)
                    dve.tensor_reduce(neg_max[:, b % 2, i * HG:(i + 1) * HG],
                                      a_bank[n % 2][:, :].rearrange("p (j s) -> p j s", s=P),
                                      AX.X, ALU.max, negate=True).then_inc(a_free, 1)
                    if i == UNITS - 1:
                        dve.wait_ge(a_free, n + 1)
                        m = neg_max[:, b % 2, :].rearrange("p (j i) -> p i j", j=HG)
                        if layer or b:
                            lb = layer * BATCHES + b - 1
                            wait_full(dve, MISC_USE[("mT", lb // BATCHES, lb % BATCHES)])
                        chained(dve.tensor_copy(by_head[:, :, :, ROW_MAX], m))
                        dve.tensor_tensor(by_head[:, :, :, ROW_MAX + 1], m, f32(by_head[:, :, :, ROW_MAX]),
                                          ALU.subtract).then_inc(max_ready, 1)
                elif kind == "pT":
                    src, n = misc(piece)
                    wait_full(dve, n)
                    pv = src[:, :].rearrange("p (h e) -> p h e", e=HW)
                    chained(dve.reciprocal(rec[:, :], pv[:, :, HD]))
                    dve.tensor_tensor(attn[:, :].rearrange("p (h e) -> p h e", e=HD), pv[:, :, 0:HD],
                                      rec[:, :].unsqueeze(2).broadcast_to([P, HEADS, HD]), ALU.mult)\
                        .then_inc(done(n), 1)
                elif kind == "wo":
                    src, n = misc(piece)
                    wait_full(dve, n)
                    if b % GROUP == 0:
                        dve.wait_ge(bo_added, layer * GROUPS + b // GROUP + 1)
                    dve.tensor_tensor(X[:, b, :], src[:, 0:P], X[:, b, :], ALU.add).then_inc(done(n), 1)
                    if b % GROUP == GROUP - 1:
                        wait_done(dve, piece)
                elif kind == "lg":
                    src, n = misc(piece)
                    wait_full(dve, n)
                    logit_src = src[:, 0:GROUP * EXPERTS].rearrange("p (b e) -> p b e", e=EXPERTS)
                    if layer == 1:
                        ins = dve.tensor_tensor(logits[:, :, :], logit_src,
                                                bg_all[:, :].unsqueeze(1).broadcast_to([P, GROUP, EXPERTS]), ALU.add)
                    else:
                        ins = dve.tensor_copy(logits[:, :, :], logit_src)
                    ins.then_inc(done(n), 1)
                    wait_done(dve, piece)
                    chained(dve.tensor_reduce(top, logits[:, :, :], AX.X, ALU.max))
                    dve.tensor_tensor(shifted[:, :, :], logits[:, :, :], over_experts(top), ALU.subtract)\
                       .then_inc(shifted_ready, 1)
                    dve.tensor_tensor(cmp_ge[:, :, :, :],
                                      logits[:, :, :].unsqueeze(2).broadcast_to([P, GROUP, EXPERTS, EXPERTS]),
                                      logits[:, :, :].unsqueeze(3).broadcast_to([P, GROUP, EXPERTS, EXPERTS]),
                                      ALU.is_ge).then_inc(compared, 1)
                elif kind == "lg2":
                    dve.wait_ge(before_ready, layer * GROUPS + g + 1)
                    ins = dve.tensor_reduce(rank[:, :, :], before[:, :, :, :], AX.X, ALU.add)
                    dve.wait_ge(exp_ready, layer * GROUPS + g + 1)
                    weight = expd
                    if layer == 1:
                        chained(dve.tensor_reduce(total, expd[:, :, :], AX.X, ALU.add))
                        chained(dve.reciprocal(rtotal, total))
                        chained(dve.tensor_tensor(shifted[:, :, :], expd[:, :, :], over_experts(rtotal), ALU.mult))
                        weight = shifted
                    else:
                        chained(ins)
                    chained(dve.scalar_tensor_tensor(out=numer[:, :, :], in0=rank[:, :, :], scalar=1.5,
                                                     in1=weight[:, :, :], op0=ALU.is_lt, op1=ALU.mult))
                elif kind == "lg3":
                    chained(dve.tensor_reduce(picked, numer[:, :, :], AX.X, ALU.add))
                    chained(dve.tensor_scalar(guarded, picked, GATE_EPS, None, ALU.max))
                    chained(dve.reciprocal(rpicked, guarded))
                    dve.tensor_tensor(gates[:, :, :], numer[:, :, :], over_experts(rpicked), ALU.mult)\
                       .then_inc(gates_ready, 1)
                elif kind == "acc":
                    src, n = misc(piece)
                    wait_full(dve, n)
                    dve.tensor_tensor(X[:, bs, :], src[:, :].rearrange("p (b d) -> p b d", d=P), X[:, bs, :],
                                      ALU.add).then_inc(done(n), 1)
                    wait_done(dve, piece)

            def slot_pieces(it, k, c):
                if isinstance(it, int):
                    for piece in SLOTS[layer].get((it, k, c), ()):
                        run(piece)

            for layer in range(LAYERS):
                for piece in ORDER[layer]:
                    run(piece)
                per = 2 * GROUPS

                def split_hidden(it, slot, g, c):
                    u = slot * GROUPS + g
                    n = layer * HPL + u * FC + c
                    dve.wait_ge(h_free, it * (per * FC) + (n + 1 + H_BANKS))
                    dve.tensor_copy(hidden_part(0, u % 2)[:, c, :], hidden[:, c % 2, :]).then_inc(hh_ready, 1)
                    if c % 2 == 0:
                        dve.wait_ge(hh_ready, it * (per * FC) + (n + 1))
                        dve.tensor_tensor(hidden_part(1, u % 2)[:, c, :], hidden[:, c % 2, :],
                                          f32(hidden_part(0, u % 2)[:, c, :]), ALU.subtract).then_inc(hl_ready, 1)

                def weigh_output(it, slot, g):
                    u = slot * GROUPS + g
                    dve.wait_ge(y_full, it * per + (layer * YPL + u + 1))
                    dve.wait_ge(gate_all_ready[u % 2], it * (16 * GROUPS) + 16 * (layer * YPL // 2 + u // 2 + 1))
                    dve.wait_ge(acc_ready, it * per + (layer * (YPL + 1) + u + 0))
                    column = cols[:, bass.ds(it * 2 + (B2_ROW + layer * EXPERTS + slot), 1)]
                    dve.scalar_tensor_tensor(out=weighted[:, u % 2, :], in0=y_bank[u % 2][:, :], scalar=column,
                                             in1=gate_all[:, u % 2, :], op0=ALU.add, op1=ALU.mult).then_inc(y_free, 1)

                def expert_pair(it):
                    units = [(it, slot, g) for slot in range(2) for g in range(GROUPS)]
                    follow = units[1:] + ([] if isinstance(it, int) and it == EXPERTS // 2 - 1 else [(it + 1, 0, 0)])
                    for k, unit in enumerate(units):
                        for c in range(FC):
                            if k < len(follow):
                                split_hidden(*follow[k], c)
                            slot_pieces(it, k, c)
                        weigh_output(*unit)
                        if k % GROUPS in (1, 2) and not (k >= GROUPS and len(follow) < len(units) and layer + 1 == LAYERS):
                            matrix, ahead = k % GROUPS - 1, k // GROUPS
                            dve.wait_ge(w_hi_ready, it * 4 + (layer * 2 * EXPERTS + 3 + 2 * ahead + matrix))
                            split_weights(matrix, 1 - ahead)

                for c in range(FC):
                    split_hidden(0, 0, 0, c)
                    slot_pieces(0, -1, c)
                expert_pair(0)
                with dve.Fori(1, EXPERTS // 2 - 1) as it:
                    expert_pair(it)
                expert_pair(EXPERTS // 2 - 1)
                if layer + 1 == LAYERS:
                    run(("acc", layer, GROUPS - 1))


LNS = [p for p in SEQUENCE if p[0] in ("ln1a", "ln2a")]
LN_INDEX = {p: n for n, p in enumerate(LNS)}
SPLITS = [p for p in SEQUENCE if p[0] in ("kp", "qp")]
SPLIT_INDEX = {p: n for n, p in enumerate(SPLITS)}
N_SMALL = 3 * LAYERS + 1
ZERO_SEL = 4
ZERO_EXTRA = ZERO_SEL + 1
N_CONST = ZERO_EXTRA + 3


def kernel(**inputs):
    import concourse.bacc as bacc
    from concourse.bass_utils import run_bass_kernel_spmd

    nc = bacc.Bacc("TRN2", target_bir_lowering=False, num_devices=1)
    arrays, aps = {}, {}
    for name, value in inputs.items():
        a = np.ascontiguousarray(value)
        arrays[f"in_{name}"] = a
        aps[name] = nc.dram_tensor(f"in_{name}", a.shape, mybir.dt.from_np(a.dtype), kind="ExternalInput").ap()
    out = nc.dram_tensor("out_x", (BATCHES, P, P), F32, kind="ExternalOutput").ap()

    def both(part, names):
        return [[aps[f"L{layer}_{part}_{n}"] for n in names] for layer in range(LAYERS)]

    def each(name):
        return [aps[f"L{layer}_{name}"] for layer in range(LAYERS)]

    gates_dram = [nc.dram_tensor(f"gates{layer}", (EXPERTS, TOKENS), F32).ap() for layer in range(LAYERS)]
    build(nc, gates_dram, aps["x"], aps["ctx_1024"], aps["condB_tau"], aps["fside_BxS2_0"],
          both("xcond", ("Wq", "Wk", "Wv", "Wo")), each("ffn_b1"), both("xcond", ("bq", "bk")),
          each("xcond_bv"), each("xcond_bo"), each("ffn_Wg"), aps["L1_ffn_bg"], each("ffn_W1"), each("ffn_W2"),
          each("ffn_b2"), out)
    r = run_bass_kernel_spmd(nc, [arrays], core_ids=[0])
    return r.results[0]["out_x"]
```
